# Optimizing a Trainium2 kernel written in Bass

```python
import numpy as np
import jax
import jax.numpy as jnp

def _softmax(x, axis=-1):
    return jax.nn.softmax(x, axis=axis)

def _gelu(x):
    return jax.nn.gelu(x, approximate=True)

def _silu(x):
    return jax.nn.silu(x)

def _sigmoid(x):
    return jax.nn.sigmoid(x)

def _layernorm(x, axis=-1, eps=1e-05):
    m = jnp.mean(x, axis=axis, keepdims=True)
    v = jnp.var(x, axis=axis, keepdims=True)
    return (x - m) / jnp.sqrt(v + eps)

def _scatter_add(tgt, idx, src, axis=0):
    return tgt.at[idx].add(src)

def _segment_sum(src, seg, n):
    return jax.ops.segment_sum(src, seg, n)
kernel_name = 'mk_gnn_preln_d2_gnn_r8_53ac95'

def setup_inputs(seed: int=0):
    np.random.seed(seed)
    _w = jnp.asarray

    def _rec_inputs():
        import jax
        import jax.numpy as jnp
        _gk = jax.random.key(seed)
        x = -0.0003713 + 1 * jax.random.normal(jax.random.fold_in(_gk, 1), (6250, 256), jnp.float32)
        _s = jax.random.randint(jax.random.fold_in(_gk, 2), (100000,), 0, 6250, jnp.int32)
        _d = jax.random.randint(jax.random.fold_in(_gk, 3), (100000,), 0, 6250, jnp.int32)
        _loop = jnp.arange(6250, dtype=jnp.int32)
        src = jnp.concatenate([_s, _d, _loop])
        dst = jnp.concatenate([_d, _s, _loop])
        _o = jnp.argsort(dst, stable=True)
        src = src[_o]
        dst = dst[_o]
        edge_attr_64 = 0.000189758 + 1.00013 * jax.random.normal(jax.random.fold_in(_gk, 12), (206250, 64), jnp.float32)
        return (x, src, dst, edge_attr_64)
    x, src, dst, edge_attr_64 = _rec_inputs()

    def _L0_gnn_setup():
        import jax, jax.numpy as jnp
        import numpy as np
        N_NODES = 6250
        N_EDGES = 100000
        NODE_DIM = 256
        EDGE_DIM = 64
        HIDDEN = 512
        OUT_DIM = 256
        key = jax.random.key(seed)
        ks = jax.random.split(key, 6)
        node_features = jax.random.normal(ks[0], (N_NODES, NODE_DIM), dtype=jnp.float32)
        edge_index = jax.random.randint(ks[1], (2, N_EDGES), 0, N_NODES, dtype=jnp.int64)
        edge_features = jax.random.normal(ks[2], (N_EDGES, EDGE_DIM), dtype=jnp.float32)
        in_dim = EDGE_DIM + NODE_DIM
        W1 = jax.random.normal(ks[3], (in_dim, HIDDEN), dtype=jnp.float32) * (1.0 / np.sqrt(in_dim))
        b1 = jnp.zeros((HIDDEN,), dtype=jnp.float32)
        W2 = jax.random.normal(ks[4], (HIDDEN, OUT_DIM), dtype=jnp.float32) * (1.0 / np.sqrt(HIDDEN))
        b2 = jnp.zeros((OUT_DIM,), dtype=jnp.float32)
        return {'node_features': node_features, 'edge_index': edge_index, 'edge_features': edge_features, 'W1': W1, 'b1': b1, 'W2': W2, 'b2': b2}
    _L0_gnn_all = _L0_gnn_setup()
    _L0_gnn_in = {k: v for k, v in _L0_gnn_all.items() if k in ('W1', 'b1', 'W2', 'b2')}
    del _L0_gnn_all

    def _L1_gnn_setup():
        import jax, jax.numpy as jnp
        import numpy as np
        N_NODES = 12500
        N_EDGES = 200000
        D_IN = 256
        D_OUT = 256
        key = jax.random.key(seed)
        k1, k2, k3, k4, k5 = jax.random.split(key, 5)
        feat = jax.random.normal(k1, (N_NODES, D_IN), dtype=jnp.float32)
        src = jax.random.randint(k2, (N_EDGES,), 0, N_NODES, dtype=jnp.int32)
        dst = jax.random.randint(k3, (N_EDGES,), 0, N_NODES, dtype=jnp.int32)
        gain = float(np.sqrt(2.0))
        limit = gain * float(np.sqrt(6.0 / (D_IN + D_OUT)))
        w_neigh = jax.random.uniform(k4, (D_OUT, D_IN), minval=-limit, maxval=limit, dtype=jnp.float32)
        w_self = jax.random.uniform(k5, (D_OUT, D_IN), minval=-limit, maxval=limit, dtype=jnp.float32)
        b_self = jnp.zeros((D_OUT,), dtype=jnp.float32)
        return {'feat': feat, 'src': src, 'dst': dst, 'w_neigh': w_neigh, 'w_self': w_self, 'b_self': b_self}
    _L1_gnn_all = _L1_gnn_setup()
    _L1_gnn_in = {k: v for k, v in _L1_gnn_all.items() if k in ('w_neigh', 'w_self', 'b_self')}
    del _L1_gnn_all
    return {'x': x, 'src': src, 'dst': dst, 'edge_attr_64': edge_attr_64, 'L0_gnn_W1': _L0_gnn_in['W1'], 'L0_gnn_b1': _L0_gnn_in['b1'], 'L0_gnn_W2': _L0_gnn_in['W2'], 'L0_gnn_b2': _L0_gnn_in['b2'], 'L1_gnn_w_neigh': _L1_gnn_in['w_neigh'], 'L1_gnn_w_self': _L1_gnn_in['w_self'], 'L1_gnn_b_self': _L1_gnn_in['b_self']}

def reference(x, src, dst, edge_attr_64, L0_gnn_W1, L0_gnn_b1, L0_gnn_W2, L0_gnn_b2, L1_gnn_w_neigh, L1_gnn_w_self, L1_gnn_b_self):
    import jax
    import jax.numpy as jnp

    def _L0_gnn_ref(node_features, edge_index, edge_features, W1, b1, W2, b2):
        import jax, jax.numpy as jnp
        import numpy as np
        N_NODES = 6250
        N_EDGES = 100000
        NODE_DIM = 256
        EDGE_DIM = 64
        HIDDEN = 512
        OUT_DIM = 256
        tgt = edge_index[1]
        agg = jax.ops.segment_sum(edge_features, tgt, num_segments=N_NODES)
        counts = jax.ops.segment_sum(jnp.ones((edge_features.shape[0],), edge_features.dtype), tgt, num_segments=N_NODES)
        agg = agg / jnp.maximum(counts, 1.0)[:, None]
        combined = jnp.concatenate([agg, node_features], axis=1)
        h = jax.nn.relu(combined @ W1 + b1)
        out = h @ W2 + b2
        return out

    def _L1_gnn_ref(feat, src, dst, w_neigh, w_self, b_self):
        import jax, jax.numpy as jnp
        import numpy as np
        N_NODES = 12500
        N_EDGES = 200000
        D_IN = 256
        D_OUT = 256
        n = feat.shape[0]
        summed = jax.ops.segment_sum(feat[src], dst, num_segments=n)
        deg = jax.ops.segment_sum(jnp.ones_like(dst, dtype=feat.dtype), dst, num_segments=n)
        h_neigh_raw = summed / jnp.maximum(deg, 1.0)[:, None]
        h_neigh = h_neigh_raw @ w_neigh.T
        rst = feat @ w_self.T + b_self + h_neigh
        return rst
    edge_index = jnp.stack([src, dst])
    h = jnp.maximum(_layernorm(x, axis=-1), 0.0)
    x = x + _L0_gnn_ref(h, edge_index, edge_attr_64, L0_gnn_W1, L0_gnn_b1, L0_gnn_W2, L0_gnn_b2)
    h = jnp.maximum(_layernorm(x, axis=-1), 0.0)
    x = x + _L1_gnn_ref(h, src, dst, L1_gnn_w_neigh, L1_gnn_w_self, L1_gnn_b_self)
    return x

_drawn_inputs = setup_inputs


def setup_inputs(seed=0):
    import zlib

    import numpy as np

    out = dict(_drawn_inputs(seed))
    spreads = {'L0_gnn_b1': (0.0, 0.1), 'L0_gnn_b2': (0.0, 0.1), 'L1_gnn_b_self': (0.0, 0.1)}
    factors = {}
    for name, (base, spread) in spreads.items():
        noise = np.random.default_rng([zlib.crc32(name.encode()), seed]).standard_normal(out[name].shape)
        drawn = base * np.exp(spread * noise) if base else spread * noise
        out[name] = jnp.asarray(drawn.astype(out[name].dtype))
    for name, factor in factors.items():
        out[name] = (out[name] * factor).astype(out[name].dtype)
    return out
```

```python
from contextlib import ExitStack

import numpy as np

import concourse.bass as bass
from concourse import mybir
from concourse.alu_op_type import AluOpType as ALU

ACT = mybir.ActivationFunctionType
AX = mybir.AxisListType
F32 = mybir.dt.float32
F16 = mybir.dt.float16
BF16 = mybir.dt.bfloat16
I32 = mybir.dt.int32
U32 = mybir.dt.uint32

P = 128


def gnn_kernel(nc, x, src, dst, edges, w1, b1, w2, b2, wneighT, wselfT, bself, out):
    N, D = x.shape
    E, FE = edges.shape
    HID = w1.shape[1]
    DH = D // P
    HB = HID // P
    CH = 8
    GE = CH * P
    G = -(-E // GE)
    GF = G - 1
    REPEATED = GF * GE - (E - GE)
    G0 = min(G, P)
    G1 = G - G0
    T = 2 * (-(-N // (2 * P)))
    NP = T * P
    TF = N // P
    REST = N - TF * P
    U = T // 2
    WIN = 48
    NW = -(-N // WIN)
    PAIRS = G // 2
    NM = 2 * P
    SCALE = 2048.0
    EPS = 1e-5
    assert G % 2 == 0 and G1 < P and PAIRS > T and U % 2 == 1 and FE == 64 and NP >= N + WIN

    ctx = ExitStack()
    with ctx:
        def sb(name, shape, dt):
            return ctx.enter_context(nc.sbuf_tensor(name, shape, dt))

        def sem(name):
            return ctx.enter_context(nc.semaphore(name))

        def sems(name):
            return [sem(f"{name}{q}") for q in range(2)]

        table = nc.dram_tensor("h1_table", (NP, 2 * D), F16).ap()

        xr = sb("xr", [P, T, D], F32)
        sumT = sb("sumT", [P, DH, NP], F32)
        acc = sb("acc", [P, NP], F32)
        rs1 = sb("rs1", [P, T], F32)
        nm1 = sb("nm1", [P, T], F32)
        invT = sb("invT", [P, T], F32)
        relT = sb("relT", [P, G, CH], F32)
        dstT = sb("dstT", [P, G, CH], F32)
        srcT = sb("srcT", [P, G, CH], U32)
        base = sb("base", [1, G], I32)
        flag = sb("flag", [1, 1], I32)
        w1a = sb("w1a", [FE, HID], F32)
        w1b = sb("w1b", [P, DH, HID], F32)
        w2s = sb("w2s", [P, HB, D], F32)
        wns = sb("wns", [P, DH, D], F32)
        wss = sb("wss", [P, DH, D], F32)
        b1T = sb("b1T", [P, HB], F32)
        b2bc = sb("b2bc", [P, D], F32)
        bsbc = sb("bsbc", [P, D], F32)
        ident = sb("ident", [P, P], F32)
        ones = sb("ones", [P, FE], F32)
        iota = sb("iota", [P, WIN], F32)
        edg = sb("edg", [P, 2, CH, FE], F32)
        oneh = sb("oneh", [P, 2, CH, WIN], F32)
        ohsum = sb("ohsum", [P, 2, WIN], F32)
        rows = sb("rows", [P, 2, CH, 2 * D], F16)
        oneb = oneh[:, :, :, :].rearrange("p q c w -> p (q c w)").bitcast(BF16)[:, 0:2 * CH * WIN].rearrange(
            "p (q c w) -> p q c w", q=2, c=CH)
        stage = sb("stage", [P, 2, CH], U32)
        hbuf = sb("hbuf", [P, 2, 2, D], F32)
        tabs = sb("tabs", [P, 2, 2, 2 * D], F16)
        hids = sb("hids", [P, 2, HB, NM], F32)
        inv64 = sb("inv64", [FE, 2, NM], F32)
        aggn = sb("aggn", [FE, 2, NM], F32)
        st6 = sb("st6", [P, 2, 2, 6], F32)
        mv = sb("mv", [P, 2, 2, 2], F32)
        ve = sb("ve", [P, 2, 2], F32)
        sd = sb("sd", [P, 2, 2], F32)
        rsq = sb("rsq", [P, 2, 2], F32)
        nmq = sb("nmq", [P, 2, 2], F32)
        tab32 = tabs[:, :, :, :].rearrange("p q t d -> p (q t d)").bitcast(F32)
        st0 = tab32[:, 0:6 * T].rearrange("p (t s) -> p t s", s=6)
        ln0 = tab32[:, 6 * T:12 * T].rearrange("p (k t) -> p k t", k=6)
        viol = sb("viol", [P, 8], F32)
        wstart = sb("wstart", [P, 1], F32)
        relw = sb("relw", [P, CH], F32)
        raw = rows[:, :, :, :].rearrange("p a c d -> p (a c d)").bitcast(F32).rearrange(
            "p (k b j) -> p k b j", k=2, b=2)
        rawi = rows[:, :, :, :].rearrange("p a c d -> p (a c d)").bitcast(I32).rearrange(
            "p (k b j) -> p k b j", k=2, b=2)
        relr = hids[:, :, :, :].rearrange("p a b n -> p (a b n)").rearrange("p (b j) -> p b j", b=2)

        bank = [ctx.enter_context(nc.psum_tensor(f"bank{n}", [P, 512], F32)) for n in range(8)]

        s_raw = sem("s_raw")
        s_x = sem("s_x")
        s_w = sem("s_w")
        s_const = sem("s_const")
        s_rawf = sem("s_rawf")
        s_viol = sem("s_viol")
        s_violT = sem("s_violT")
        s_flag = sem("s_flag")
        s_idx_tr = sem("s_idx_tr")
        s_idx_act = sem("s_idx_act")
        s_idx_dve = sem("s_idx_dve")
        s_masked = sem("s_masked")
        s_var0 = sem("s_var0")
        s_sd0 = sem("s_sd0")
        s_ln0 = sem("s_ln0")
        s_h0 = sems("s_h0_")
        s_h0tr = sems("s_h0tr_")
        s_h0T = sems("s_h0T_")
        s_b2 = sem("s_b2")
        s_edges = sems("s_edges_")
        s_oneh = sems("s_oneh_")
        s_ohsum = sems("s_ohsum_")
        s_esum = sems("s_esum_")
        s_added = sems("s_added_")
        s_inv = sem("s_inv")
        s_agg = sems("s_agg_")
        s_hidp = sems("s_hidp_")
        s_hids = sems("s_hids_")
        s_invp = sems("s_invp_")
        s_outp = sems("s_outp_")
        s_x1 = sems("s_x1_")
        s_var1 = sems("s_var1_")
        s_sd1 = sems("s_sd1_")
        s_ln1 = sems("s_ln1_")
        s_hi = sems("s_hi_")
        s_tab = sems("s_tab_")
        s_stored = sems("s_stored_")
        s_zero = sem("s_zero")
        s_stage = sems("s_stage_")
        s_rows = sems("s_rows_")
        s_oneb = sems("s_oneb_")
        s_nsum = sems("s_nsum_")
        s_nadded = sems("s_nadded_")
        s_self_h = sem("s_self_h")
        s_self_tr = sem("s_self_tr")
        s_self_T = sem("s_self_T")
        s_self_p = sem("s_self_p")
        s_self = sem("s_self")
        s_sumc = sems("s_sumc_")
        s_neighp = sems("s_neighp_")
        s_res = sems("s_res_")
        s_out = sems("s_out_")
        a_edges = sem("a_edges")
        a_oneh = sem("a_oneh")
        a_sum = sem("a_sum")
        a_added = sem("a_added")
        a_group = sem("a_group")
        n_stage = sem("n_stage")
        n_rows = sem("n_rows")
        n_oneb = sem("n_oneb")
        n_sum = sem("n_sum")
        n_group = sem("n_group")

        def edge_rows(g):
            return edges[bass.ds(g * GE, GE), :].rearrange("(p c) f -> p (c f)", c=CH)

        last_edge_rows = edges[E - GE:E, :].rearrange("(p c) f -> p (c f)", c=CH)

        def fast(eng):
            eng.wait_ge(s_flag, 1)
            return eng.value_load(flag[0:1, 0:1], min_val=0, max_val=1) < 1

        def loop(eng, body, first, end, step=1):
            with eng.Fori(first, end, step) as i:
                body(i)

        block = ctx.enter_context(nc.Block())

        @block.sync
        def _(sp):
            for k, v in enumerate((dst, src)):
                sp.dma_start(rawi[0:G0, k, 0, :], v[0:G0 * GE].rearrange("(g j) -> g j", g=G0)).then_inc(s_raw, 16)
                sp.dma_start(rawi[0:G1 - 1, k, 1, :],
                             v[G0 * GE:GF * GE].rearrange("(g j) -> g j", g=G1 - 1)).then_inc(s_raw, 16)
                sp.dma_start(rawi[G1 - 1:G1, k, 1, :], v[E - GE:E].rearrange("(g j) -> g j", g=1)).then_inc(s_raw, 16)
            with nc.allow_non_contiguous_dma(reason="one index of each group"):
                sp.dma_start(base[0:1, 0:GF], dst[0:GF * GE].rearrange("(g j) -> j g", g=GF)[0:1, :]).then_inc(s_raw, 16)
            sp.dma_start(base[0:1, GF:G], dst[E - GE:E - GE + 1].rearrange("(a b) -> a b", a=1)).then_inc(s_raw, 16)
            sp.wait_ge(s_const, 1)
            step = 8
            for t in range(0, TF, step):
                m = min(step, TF - t)
                sp.dma_start(xr[:, t:t + m, :], x[t * P:(t + m) * P, :].rearrange("(t p) d -> p t d", p=P)).then_inc(s_x, 16)
            sp.dma_start(xr[0:REST, TF, :], x[TF * P:N, :]).then_inc(s_x, 16)
            sp.dma_start(w1a[:, :], w1[0:FE, :]).then_inc(s_w, 16)
            sp.dma_start(w1b[:, :, :], w1[FE:FE + D, :].rearrange("(h p) n -> p h n", p=P)).then_inc(s_w, 16)
            sp.dma_start(w2s[:, :, :], w2.rearrange("(h p) n -> p h n", p=P)).then_inc(s_w, 16)
            sp.dma_start(wns[:, :, :], wneighT.rearrange("(h p) n -> p h n", p=P)).then_inc(s_w, 16)
            sp.dma_start(wss[:, :, :], wselfT.rearrange("(h p) n -> p h n", p=P)).then_inc(s_w, 16)
            with nc.allow_non_contiguous_dma(reason="a bias on the partitions"):
                sp.dma_start(b1T[:, :], b1.rearrange("(h p) -> p h", p=P)).then_inc(s_w, 16)
            sp.dma_start(b2bc[:, :], b2.rearrange("(a n) -> a n", a=1).broadcast_to([P, D])).then_inc(s_w, 16)
            sp.dma_start(bsbc[:, :], bself.rearrange("(a n) -> a n", a=1).broadcast_to([P, D])).then_inc(s_w, 16)

            with sp.If(fast(sp)):
                def load(i, q, rows_of=None):
                    if not isinstance(i, int) or i:
                        sp.wait_ge(s_esum[q], i)
                    sp.dma_start(edg[:, q, :, :].rearrange("p c f -> p (c f)"),
                                 edge_rows(2 * i + q) if rows_of is None else rows_of).then_inc(s_edges[q], 16)

                def both(i):
                    load(i, 0)
                    load(i, 1)

                both(0)
                loop(sp, both, 1, PAIRS - 1)
                load(PAIRS - 1, 0)
                load(PAIRS - 1, 1, last_edge_rows)
            with sp.Else():
                def load_any(g, rows_of=None):
                    if not isinstance(g, int) or g:
                        sp.wait_ge(a_group, g)
                    sp.dma_start(edg[:, 0, :, :].rearrange("p c f -> p (c f)"),
                                 edge_rows(g) if rows_of is None else rows_of).then_inc(a_edges, 16)

                load_any(0)
                loop(sp, load_any, 1, GF)
                load_any(GF, last_edge_rows)

            def store(i, q):
                u = 2 * i + q
                sp.wait_ge(s_tab[q], i + 1)
                sp.dma_start(table[bass.ds(u * NM, NM), :].rearrange("(t p) d -> p t d", p=P),
                             tabs[:, q, :, :]).then_inc(s_stored[q], 16)

            def two(i):
                store(i, 0)
                store(i, 1)

            loop(sp, two, 0, U // 2)
            store(U // 2, 0)

            def result(i, q, n=P):
                t = 2 * i + q
                sp.wait_ge(s_res[q], i + 1)
                sp.dma_start(out[bass.ds(t * P, n), :], hbuf[0:n, q, 0, :]).then_inc(s_out[q], 16)

            def two_results(i):
                result(i, 0)
                result(i, 1)

            loop(sp, two_results, 0, TF // 2)
            result(TF // 2, 0, REST)
            sp.wait_ge(s_out[0], 16 * (TF // 2 + 1))
            sp.wait_ge(s_out[1], 16 * (TF // 2))

        @block.gpsimd
        def _(pool):
            pool.memset(xr[:, TF:T, :], 0.0).then_inc(s_const, 1)
            pool.memset(ident[:, :], 0.0)
            pool.memset(ones[:, :], 1.0)
            pool.memset(viol[:, :], 0.0)
            pool.memset(acc[:, :], 0.0)
            pool.iota(iota[:, :], pattern=[[1, WIN]], base=0, channel_multiplier=0,
                      allow_small_or_imprecise_dtypes=True)
            pool.drain()
            pool.affine_select(out=ident[:, :], in_=ident[:, :], compare_op=ALU.not_equal, fill=1.0,
                               base=0, pattern=[[-1, P]], channel_multiplier=1).then_inc(s_const, 1)
            pool.wait_ge(s_idx_act, 2 * CH)
            for v in (relT, dstT):
                pool.affine_select(out=v[:, GF, :], in_=v[:, GF, :], compare_op=ALU.is_ge, fill=-1.0,
                                   base=-REPEATED, pattern=[[1, CH]], channel_multiplier=CH).then_inc(s_masked, 1)
            pool.wait_ge(s_masked, 2)

            def add_b2(i, q):
                pool.wait_ge(s_h0[q], i + 1)
                v = xr[:, bass.ds(2 * (2 * i + q), 2), :]
                pool.tensor_tensor(v, v, b2bc[:, :].unsqueeze(1).broadcast_to([P, 2, D]), ALU.add).then_inc(s_b2, 1)

            pool.wait_ge(s_w, 8 * 16)
            def two(i):
                add_b2(i, 0)
                add_b2(i, 1)

            loop(pool, two, 0, U // 2)
            add_b2(U // 2, 0)

            def table_stored():
                pool.wait_ge(s_stored[0], 16 * (U // 2 + 1))

            table_stored()
            pool.wait_ge(s_stored[1], 16 * (U // 2))

            def gather(q, done):
                for c in range(CH):
                    pool.indirect_dma_start(rows[:, q, c, :], None, table,
                                            bass.IndirectOffsetOnAxis(ap=stage[:, q, c:c + 1], axis=0)).then_inc(done, 16)

            with pool.If(fast(pool)):
                def group(n, q):
                    table_stored()
                    pool.wait_ge(s_stage[q], n)
                    gather(q, s_rows[q])

                def both2(i):
                    group(i, 0)
                    group(i, 1)

                loop(pool, both2, 1, PAIRS + 1)
            with pool.Else():
                def any_group(n):
                    table_stored()
                    pool.wait_ge(n_stage, n)
                    gather(0, n_rows)

                loop(pool, any_group, 1, G + 1)

        @block.scalar
        def _(act):
            for c in range(CH):
                for k, v in enumerate((relT, dstT)):
                    act.wait_ge(s_idx_tr, 3 * c + k + 1)
                    act.activation(v[:, :, c], bank[2 * k + c % 2][:, 0:G], ACT.Copy).then_inc(s_idx_act, 1)
            act.wait_ge(s_var0, 1)
            act.activation(ln0[:, 3, :], ln0[:, 1, :], ACT.Sqrt).then_inc(s_sd0, 1)
            act.wait_ge(s_ln0, 1)

            def h0(i, q):
                u = 2 * i + q
                if not isinstance(i, int) or i:
                    act.wait_ge(s_h0tr[q], i)
                for t in range(2):
                    ins = act.activation(hbuf[:, q, t, :], xr[:, bass.ds(2 * u + t, 1), :].rearrange("p a d -> p (a d)"),
                                         ACT.Relu, bias=ln0[:, 5, bass.ds(2 * u + t, 1)], scale=ln0[:, 4, bass.ds(2 * u + t, 1)])
                ins.then_inc(s_h0[q], 1)

            def h0T(i, q):
                u = 2 * i + q
                act.wait_ge(s_h0tr[q], i + 1)
                act.activation(sumT[:, :, bass.ds(u * NM, NM)],
                               bank[3 + q][:, :].rearrange("p (h n) -> p h n", h=DH), ACT.Copy).then_inc(s_h0T[q], 1)

            def both(i):
                h0(i, 0)
                h0(i, 1)
                h0T(i, 0)
                h0T(i, 1)

            both(0)
            loop(act, both, 1, U // 2)
            h0(U // 2, 0)
            h0T(U // 2, 0)

            def hidden(i, q):
                if not isinstance(i, int) or i:
                    act.wait_ge(s_outp[q], i)
                for k in range(2):
                    act.wait_ge(s_hidp[q], 2 * i + k + 1)
                    for b in range(2):
                        ins = act.activation(hids[:, q, 2 * k + b, :], bank[3 + 2 * q + k][:, b * NM:(b + 1) * NM],
                                             ACT.Relu, bias=b1T[:, 2 * k + b:2 * k + b + 1])
                    ins.then_inc(s_hids[q], 1)

            def sd_of(i, q):
                act.wait_ge(s_var1[q], i + 1)
                act.activation(sd[:, q, :], ve[:, q, :], ACT.Sqrt).then_inc(s_sd1[q], 1)

            def h1(i, q):
                u = 2 * i + q
                act.wait_ge(s_ln1[q], i + 1)
                if not isinstance(i, int) or i:
                    act.wait_ge(s_stored[q], 16 * i)
                for t in range(2):
                    act.activation(hbuf[:, q, t, :], xr[:, bass.ds(2 * u + t, 1), :].rearrange("p a d -> p (a d)"),
                                   ACT.Relu, bias=nmq[:, q, t:t + 1], scale=rsq[:, q, t:t + 1])
                act.drain()
                act.activation(tabs[:, q, :, 0:D], hbuf[:, q, :, :], ACT.Copy).then_inc(s_hi[q], 1)

            def layer0(i):
                hidden(i, 0)
                hidden(i, 1)
                for q in range(2):
                    sd_of(i, q)
                for q in range(2):
                    h1(i, q)

            layer0(0)
            loop(act, layer0, 1, U // 2)
            hidden(U // 2, 0)
            sd_of(U // 2, 0)
            h1(U // 2, 0)

            act.wait_ge(s_tab[0], U // 2 + 1)
            act.wait_ge(s_tab[1], U // 2)

            def stage_src(i, q):
                if not isinstance(i, int) or i:
                    act.wait_ge(s_nsum[q], i)
                act.activation(stage[:, q, :], srcT[:, bass.ds(2 * i + q, 1), :].rearrange("p a c -> p (a c)"),
                               ACT.Copy).then_inc(s_stage[q], 1)

            def self_h(t):
                if not isinstance(t, int) or t:
                    act.wait_ge(s_self_tr, t)
                act.activation(hbuf[:, 0, 0, :], xr[:, bass.ds(t, 1), :].rearrange("p a d -> p (a d)"), ACT.Relu,
                               bias=nm1[:, bass.ds(t, 1)], scale=rs1[:, bass.ds(t, 1)]).then_inc(s_self_h, 1)

            def self_T(t):
                act.wait_ge(s_self_tr, t + 1)
                if not isinstance(t, int) or t:
                    act.wait_ge(s_self_p, t)
                act.activation(hbuf[:, 0, 1, :], bank[3][:, 0:D], ACT.Copy).then_inc(s_self_T, 1)

            def with_self(i):
                stage_src(i, 0)
                stage_src(i, 1)
                self_h(i)
                self_T(i)

            def without(i):
                stage_src(i, 0)
                stage_src(i, 1)

            def copy_sums(i, q):
                if not isinstance(i, int) or i:
                    act.wait_ge(s_neighp[q], i)
                act.activation(hids[:, q, 0, :].rearrange("p (h n) -> p h n", h=DH),
                               sumT[:, :, bass.ds((2 * i + q) * P, P)], ACT.Copy).then_inc(s_sumc[q], 1)

            with act.If(fast(act)):
                with_self(0)
                loop(act, with_self, 1, T)
                loop(act, without, T, PAIRS)
            with act.Else():
                def self_only(t):
                    self_h(t)
                    self_T(t)

                self_only(0)
                loop(act, self_only, 1, T)

                def any_src(g):
                    if not isinstance(g, int) or g:
                        act.wait_ge(n_group, g)
                    act.activation(stage[:, 0, :], srcT[:, bass.ds(g, 1), :].rearrange("p a c -> p (a c)"),
                                   ACT.Copy).then_inc(n_stage, 1)

                any_src(0)
                loop(act, any_src, 1, G)

            act.wait_ge(s_zero, 2)

            def two_tiles(i):
                copy_sums(i, 0)
                copy_sums(i, 1)

            two_tiles(0)
            loop(act, two_tiles, 1, TF // 2)
            copy_sums(TF // 2, 0)

        @block.tensor
        def _(pe):
            pe.wait_ge(s_const, 2)
            pe.wait_ge(s_viol, 1)
            pe.transpose(bank[7][0:1, 256:384], viol[:, 0:1], ident[:, :]).then_inc(s_violT, 1)
            for c in range(CH):
                for k, tab in enumerate((relr, raw[:, 0], raw[:, 1])):
                    if c >= 2:
                        if k < 2:
                            pe.wait_ge(s_idx_act, 2 * (c - 2) + k + 1)
                        else:
                            pe.wait_ge(s_idx_dve, c - 1)
                    for b, m in ((0, G0), (1, G1)):
                        ins = pe.transpose(bank[2 * k + c % 2][:, b * P:b * P + m],
                                           tab[0:m, b, :].rearrange("g (p c) -> g c p", c=CH)[:, c, :], ident[0:m, 0:m])
                    ins.then_inc(s_idx_tr, 1)

            def h0tr(i, q):
                pe.wait_ge(s_h0[q], i + 1)
                if isinstance(i, int) and i == 0:
                    pe.wait_ge(s_idx_act, 2 * CH)
                    pe.wait_ge(s_idx_dve, CH)
                else:
                    pe.wait_ge(s_h0T[q], i)
                for h in range(DH):
                    for t in range(2):
                        ins = pe.transpose(bank[3 + q][:, h * NM + t * P:h * NM + (t + 1) * P],
                                           hbuf[:, q, t, h * P:(h + 1) * P], ident[:, :])
                ins.then_inc(s_h0tr[q], 1)

            def both(i):
                h0tr(i, 0)
                h0tr(i, 1)

            both(0)
            loop(pe, both, 1, U // 2)
            h0tr(U // 2, 0)

            def edge_sums(into, q):
                for c in range(CH):
                    pe.matmul(into[0:FE, 0:WIN], edg[:, q, c, :], oneh[:, q, c, :], start=(c == 0), stop=(c == CH - 1))

            with pe.If(fast(pe)):
                def group(i, q):
                    pe.wait_ge(s_edges[q], 16 * (i + 1))
                    pe.wait_ge(s_oneh[q], i + 1)
                    if not isinstance(i, int) or i:
                        pe.wait_ge(s_added[q], i)
                    edge_sums(bank[q], q)
                    pe.wait_ge(s_ohsum[q], i + 1)
                    pe.matmul(bank[q][FE:P, 0:WIN], ones[:, :], ohsum[:, q, :], start=True, stop=True).then_inc(s_esum[q], 1)

                def both_groups(i):
                    group(i, 0)
                    group(i, 1)

                both_groups(0)
                loop(pe, both_groups, 1, PAIRS)
            with pe.Else():
                def any_group(g):
                    with pe.Fori(0, NW) as w:
                        pe.wait_ge(a_edges, 16 * (g + 1))
                        pe.wait_ge(a_oneh, g * NW + w + 1)
                        edge_sums(bank[0], 0)
                        pe.matmul(bank[0][FE:P, 0:WIN], ones[:, :], ohsum[:, 0, :], start=True, stop=True).then_inc(a_sum, 1)

                loop(pe, any_group, 0, G)

            pe.wait_ge(s_w, 8 * 16)
            pe.wait_ge(s_h0T[0], U // 2 + 1)
            pe.wait_ge(s_h0T[1], U // 2)

            def hidden(i, q):
                u = 2 * i + q
                pe.wait_ge(s_agg[q], i + 1)
                for k in range(2):
                    if not isinstance(i, int) or i:
                        pe.wait_ge(s_hids[q], 2 * (i - 1) + k + 1)
                    for b in range(2):
                        o = bank[3 + 2 * q + k][:, b * NM:(b + 1) * NM]
                        cols = slice((2 * k + b) * P, (2 * k + b + 1) * P)
                        pe.matmul(o, w1a[:, cols], aggn[:, q, :], start=True, stop=False)
                        for h in range(DH):
                            ins = pe.matmul(o, w1b[:, h, cols], sumT[:, h, bass.ds(u * NM, NM)], start=False, stop=(h == DH - 1))
                    ins.then_inc(s_hidp[q], 1)
                for t in range(2):
                    ins = pe.transpose(bank[1 + q][:, t * FE:(t + 1) * FE], inv64[:, q, t * P:(t + 1) * P], ident[0:FE, 0:FE])
                ins.then_inc(s_invp[q], 1)

            def outer(i, q):
                o = bank[7 * (1 - q)]
                if not isinstance(i, int) or i:
                    pe.wait_ge(s_x1[q], i)
                pe.wait_ge(s_hids[q], 2 * i + 2)
                for t in range(2):
                    for b in range(HB):
                        ins = pe.matmul(o[:, t * D:(t + 1) * D], hids[:, q, b, t * P:(t + 1) * P], w2s[:, b, :],
                                        start=(b == 0), stop=(b == HB - 1))
                ins.then_inc(s_outp[q], 1)

            def layer0(i):
                hidden(i, 0)
                hidden(i, 1)
                outer(i, 0)
                outer(i, 1)

            layer0(0)
            loop(pe, layer0, 1, U // 2)
            hidden(U // 2, 0)
            outer(U // 2, 0)

            pe.wait_ge(s_x1[0], U // 2 + 1)
            pe.wait_ge(s_x1[1], U // 2)
            pe.wait_ge(s_hids[0], 2 * (U // 2) + 2)
            def node_sums(into, q):
                for h in range(DH):
                    for c in range(CH):
                        for k in range(2):
                            ins = pe.matmul(into[:, h * WIN:(h + 1) * WIN],
                                            rows[:, q, c, k * D + h * P:k * D + (h + 1) * P], oneb[:, q, c, :],
                                            start=(c == 0 and k == 0), stop=(c == CH - 1 and k == 1))
                return ins

            def self_tr(t):
                pe.wait_ge(s_self_h, t + 1)
                if not isinstance(t, int) or t:
                    pe.wait_ge(s_self_T, t)
                for h in range(DH):
                    ins = pe.transpose(bank[3][:, h * P:(h + 1) * P], hbuf[:, 0, 0, h * P:(h + 1) * P], ident[:, :])
                ins.then_inc(s_self_tr, 1)

            def self_p(t):
                pe.wait_ge(s_self_T, t + 1)
                if not isinstance(t, int) or t:
                    pe.wait_ge(s_self, t)
                for h in range(DH):
                    ins = pe.matmul(bank[5][:, 0:D], hbuf[:, 0, 1, h * P:(h + 1) * P], wss[:, h, :],
                                    start=(h == 0), stop=(h == DH - 1))
                ins.then_inc(s_self_p, 1)

            with pe.If(fast(pe)):
                def sums(i, q):
                    pe.wait_ge(s_oneb[q], i + 1)
                    pe.wait_ge(s_rows[q], 16 * CH * (i + 1))
                    node_sums(bank[q], q).then_inc(s_nsum[q], 1)

                def with_self(i):
                    self_tr(i)
                    sums(i, 0)
                    self_p(i)
                    sums(i, 1)

                def without(i):
                    sums(i, 0)
                    sums(i, 1)

                with_self(0)
                loop(pe, with_self, 1, T)
                loop(pe, without, T, PAIRS)
            with pe.Else():
                def self_only(t):
                    self_tr(t)
                    self_p(t)

                self_only(0)
                loop(pe, self_only, 1, T)

                def any_sums(g):
                    with pe.Fori(0, NW) as w:
                        pe.wait_ge(n_rows, 16 * CH * (g + 1))
                        pe.wait_ge(n_oneb, g * NW + w + 1)
                        node_sums(bank[0], 0).then_inc(n_sum, 1)

                loop(pe, any_sums, 0, G)

            def neigh(i, q):
                pe.wait_ge(s_sumc[q], i + 1)
                if not isinstance(i, int) or i:
                    pe.wait_ge(s_res[q], i)
                for h in range(DH):
                    ins = pe.matmul(bank[3 + q][:, 0:D], hids[:, q, 0, h * P:(h + 1) * P], wns[:, h, :],
                                    start=(h == 0), stop=(h == DH - 1))
                ins.then_inc(s_neighp[q], 1)

            def two_tiles(i):
                neigh(i, 0)
                neigh(i, 1)

            two_tiles(0)
            loop(pe, two_tiles, 1, TF // 2)
            neigh(TF // 2, 0)

        @block.vector
        def _(dve):
            dve.wait_ge(s_raw, 8 * 16)
            for k in range(2):
                for b, m in ((0, G0), (1, G1)):
                    dve.tensor_copy(raw[0:m, k, b, :], rawi[0:m, k, b, :])
            dve.wait_ge(s_const, 2)
            dve.drain()
            for b, m in ((0, G0), (1, G1)):
                dve.tensor_scalar(relr[0:m, b, :], raw[0:m, 0, b, :], raw[0:m, 0, b, 0:1], None, ALU.subtract)
            dve.drain()
            for b, m in ((0, G0), (1, G1)):
                dve.tensor_reduce(viol[0:m, 2 * b + 1:2 * b + 2], relr[0:m, b, :], AX.X, ALU.max)
                dve.tensor_reduce(viol[0:m, 2 * b + 2:2 * b + 3], relr[0:m, b, :], AX.X, ALU.min)
            dve.drain()
            dve.tensor_scalar(viol[:, 5:6], viol[:, 1:2], viol[:, 3:4], float(WIN - 1), ALU.max, ALU.subtract)
            dve.tensor_scalar(viol[:, 6:7], viol[:, 2:3], viol[:, 4:5], -1.0, ALU.min, ALU.mult)
            dve.drain()
            dve.tensor_tensor(viol[:, 0:1], viol[:, 5:6], viol[:, 6:7], ALU.max).then_inc(s_viol, 1)
            dve.wait_ge(s_violT, 1)
            dve.tensor_reduce(viol[0:1, 7:8], bank[7][0:1, 256:384], AX.X, ALU.max)
            dve.drain()
            dve.tensor_scalar(flag[0:1, 0:1], viol[0:1, 7:8], 0.0, 1.0, ALU.max, ALU.min).then_inc(s_flag, 1)
            for c in range(CH):
                dve.wait_ge(s_idx_tr, 3 * c + 3)
                dve.tensor_copy(srcT[:, :, c], bank[4 + c % 2][:, 0:G]).then_inc(s_idx_dve, 1)

            dve.wait_ge(s_x, 16 * (-(-TF // 8) + 1))
            with dve.Fori(0, T) as t:
                dve.bn_stats(st0[:, bass.ds(t, 1), :].rearrange("p a s -> p (a s)"),
                             xr[:, bass.ds(t, 1), :].rearrange("p a d -> p (a d)"))
            dve.drain()
            mean, var, diff, root, rstd, nmr = (ln0[:, k, :] for k in range(6))
            dve.tensor_tensor(mean, st0[:, :, 1], st0[:, :, 4], ALU.add)
            dve.tensor_tensor(diff, st0[:, :, 1], st0[:, :, 4], ALU.subtract)
            dve.tensor_tensor(var, st0[:, :, 2], st0[:, :, 5], ALU.add)
            dve.drain()
            dve.tensor_tensor(diff, diff, diff, ALU.mult)
            dve.tensor_scalar(var, var, 1.0 / D, EPS, ALU.mult, ALU.add)
            dve.drain()
            dve.scalar_tensor_tensor(var, diff, 0.25, var, ALU.mult, ALU.add).then_inc(s_var0, 1)
            dve.wait_ge(s_sd0, 1)
            dve.reciprocal(rstd, root)
            dve.drain()
            dve.scalar_tensor_tensor(nmr, mean, -0.5, rstd, ALU.mult, ALU.mult).then_inc(s_ln0, 1)

            def add_window(into, start, part):
                v = into[..., bass.ds(start, WIN)]
                ins = dve.tensor_tensor(v, v, part, ALU.add)
                return ins

            with dve.If(fast(dve)):
                def count(i, q):
                    if not isinstance(i, int) or i:
                        dve.wait_ge(s_esum[q], i)
                    dve.tensor_tensor(oneh[:, q, :, :], iota[:, :].unsqueeze(1).broadcast_to([P, CH, WIN]),
                                      relT[:, bass.ds(2 * i + q, 1), :].rearrange("p a c -> p (a c)").unsqueeze(2).broadcast_to([P, CH, WIN]),
                                      ALU.is_equal).then_inc(s_oneh[q], 1)
                    dve.drain()
                    dve.tensor_reduce(ohsum[:, q, :], oneh[:, q, :, :].rearrange("p c w -> p w c"), AX.X,
                                      ALU.add).then_inc(s_ohsum[q], 1)

                def add(i, q):
                    start = dve.value_load(base[0:1, bass.ds(2 * i + q, 1)], min_val=0, max_val=N - 1)
                    dve.wait_ge(s_esum[q], i + 1)
                    add_window(acc[:, :], start, bank[q][:, 0:WIN]).then_inc(s_added[q], 1)
                    dve.drain()

                def both(i):
                    count(i, 0)
                    count(i, 1)
                    add(i, 0)
                    add(i, 1)

                dve.wait_ge(s_masked, 2)
                both(0)
                loop(dve, both, 1, PAIRS)
            with dve.Else():
                dve.wait_ge(s_masked, 2)
                with dve.Fori(0, G) as g:
                    dve.memset(wstart[:, :], 0.0)
                    dve.drain()
                    with dve.Fori(0, NW) as w:
                        dve.tensor_scalar(relw[:, :], dstT[:, bass.ds(g, 1), :].rearrange("p a c -> p (a c)"),
                                          wstart[:, 0:1], None, ALU.subtract)
                        dve.drain()
                        dve.tensor_scalar(wstart[:, :], wstart[:, :], float(WIN), None, ALU.add)
                        dve.tensor_tensor(oneh[:, 0, :, :], iota[:, :].unsqueeze(1).broadcast_to([P, CH, WIN]),
                                          relw[:, :].unsqueeze(2).broadcast_to([P, CH, WIN]), ALU.is_equal)
                        dve.drain()
                        dve.tensor_reduce(ohsum[:, 0, :], oneh[:, 0, :, :].rearrange("p c w -> p w c"), AX.X,
                                          ALU.add).then_inc(a_oneh, 1)
                        dve.wait_ge(a_sum, g * NW + w + 1)
                        add_window(acc[:, :], w * WIN, bank[0][:, 0:WIN])
                        dve.drain()
                    dve.nop().then_inc(a_group, 1)

            dve.tensor_scalar(acc[FE:P, :], acc[FE:P, :], 1.0, None, ALU.max)
            dve.drain()
            dve.reciprocal(acc[FE:P, :], acc[FE:P, :])
            dve.drain()

            def mean_edges(i, q):
                u = 2 * i + q
                dve.tensor_copy(inv64[:, q, :], acc[FE:P, bass.ds(u * NM, NM)])
                dve.drain()
                dve.tensor_tensor(aggn[:, q, :], acc[0:FE, bass.ds(u * NM, NM)], inv64[:, q, :], ALU.mult).then_inc(s_agg[q], 1)

            def keep_inv(i, q):
                dve.wait_ge(s_invp[q], i + 1)
                dve.tensor_scalar(invT[:, bass.ds(2 * (2 * i + q), 2)],
                                  bank[1 + q][:, 0:2 * FE].rearrange("p (t k) -> p t k", t=2)[:, :, 0],
                                  1.0 / SCALE, None, ALU.mult)

            def x1_stats(i, q):
                u = 2 * i + q
                v = xr[:, bass.ds(2 * u, 2), :]
                dve.wait_ge(s_outp[q], i + 1)
                dve.tensor_tensor(v, v, bank[7 * (1 - q)][:, :].rearrange("p (t d) -> p t d", t=2), ALU.add).then_inc(s_x1[q], 1)
                dve.drain()
                for t in range(2):
                    dve.bn_stats(st6[:, q, t, :], xr[:, bass.ds(2 * u + t, 1), :].rearrange("p a d -> p (a d)"))
                dve.drain()
                for t in range(2):
                    dve.bn_aggr(mv[:, q, t, :], st6[:, q, t, :])
                dve.drain()
                dve.tensor_scalar(ve[:, q, :], mv[:, q, :, 1], EPS, None, ALU.add).then_inc(s_var1[q], 1)

            def ln1(i, q):
                u = 2 * i + q
                dve.wait_ge(s_sd1[q], i + 1)
                dve.reciprocal(sd[:, q, :], sd[:, q, :])
                dve.drain()
                dve.tensor_scalar(rsq[:, q, :], sd[:, q, :], SCALE, None, ALU.mult)
                dve.scalar_tensor_tensor(nmq[:, q, :], mv[:, q, :, 0], -SCALE, sd[:, q, :], ALU.mult, ALU.mult).then_inc(s_ln1[q], 1)
                dve.drain()
                dve.tensor_copy(rs1[:, bass.ds(2 * u, 2)], rsq[:, q, :])
                dve.tensor_copy(nm1[:, bass.ds(2 * u, 2)], nmq[:, q, :])

            def low_part(i, q):
                dve.wait_ge(s_hi[q], i + 1)
                dve.tensor_tensor(tabs[:, q, :, D:2 * D], hbuf[:, q, :, :], tabs[:, q, :, 0:D], ALU.subtract).then_inc(s_tab[q], 1)

            dve.wait_ge(s_b2, U)
            mean_edges(0, 0)
            mean_edges(0, 1)

            def layer0(i, last=False):
                keep_inv(i, 0)
                x1_stats(i, 0)
                keep_inv(i, 1)
                mean_edges(i + 1, 0)
                if not last:
                    mean_edges(i + 1, 1)
                x1_stats(i, 1)
                ln1(i, 0)
                ln1(i, 1)
                low_part(i, 0)
                low_part(i, 1)

            loop(dve, layer0, 0, U // 2 - 1)
            layer0(U // 2 - 1, last=True)
            keep_inv(U // 2, 0)
            x1_stats(U // 2, 0)
            ln1(U // 2, 0)
            low_part(U // 2, 0)

            dve.memset(sumT[:, :, :], 0.0)
            dve.drain()

            def self_add(t):
                dve.wait_ge(s_self_p, t + 1)
                v = xr[:, bass.ds(t, 1), :].rearrange("p a d -> p (a d)")
                dve.scalar_tensor_tensor(v, bank[5][:, 0:D], 1.0 / SCALE, v, ALU.mult, ALU.add).then_inc(s_self, 1)
                dve.drain()
                dve.tensor_tensor(v, v, bsbc[:, :], ALU.add)

            with dve.If(fast(dve)):
                def one_hot(i, q):
                    if not isinstance(i, int) or i:
                        dve.wait_ge(s_nsum[q], i)
                    dve.tensor_tensor(oneb[:, q, :, :], iota[:, :].unsqueeze(1).broadcast_to([P, CH, WIN]),
                                      relT[:, bass.ds(2 * i + q, 1), :].rearrange("p a c -> p (a c)").unsqueeze(2).broadcast_to([P, CH, WIN]),
                                      ALU.is_equal).then_inc(s_oneb[q], 1)

                def add2(i, q):
                    start = dve.value_load(base[0:1, bass.ds(2 * i + q, 1)], min_val=0, max_val=N - 1)
                    dve.wait_ge(s_nsum[q], i + 1)
                    add_window(sumT[:, :, :], start, bank[q][:, 0:DH * WIN].rearrange("p (h w) -> p h w", h=DH))
                    dve.drain()

                def with_self(i):
                    one_hot(i, 0)
                    one_hot(i, 1)
                    add2(i, 0)
                    self_add(i)
                    add2(i, 1)

                def without(i):
                    one_hot(i, 0)
                    one_hot(i, 1)
                    add2(i, 0)
                    add2(i, 1)

                with_self(0)
                loop(dve, with_self, 1, T)
                loop(dve, without, T, PAIRS)
            with dve.Else():
                loop(dve, self_add, 0, T)
                with dve.Fori(0, G) as g:
                    dve.memset(wstart[:, :], 0.0)
                    dve.drain()
                    with dve.Fori(0, NW) as w:
                        dve.tensor_scalar(relw[:, :], dstT[:, bass.ds(g, 1), :].rearrange("p a c -> p (a c)"),
                                          wstart[:, 0:1], None, ALU.subtract)
                        dve.drain()
                        dve.tensor_scalar(wstart[:, :], wstart[:, :], float(WIN), None, ALU.add)
                        dve.tensor_tensor(oneb[:, 0, :, :], iota[:, :].unsqueeze(1).broadcast_to([P, CH, WIN]),
                                          relw[:, :].unsqueeze(2).broadcast_to([P, CH, WIN]), ALU.is_equal).then_inc(n_oneb, 1)
                        dve.wait_ge(n_sum, g * NW + w + 1)
                        add_window(sumT[:, :, :], w * WIN, bank[0][:, 0:DH * WIN].rearrange("p (h w) -> p h w", h=DH))
                        dve.drain()
                    dve.nop().then_inc(n_group, 1)

            dve.drain()
            dve.nop().then_inc(s_zero, 2)

            def result(i, q):
                t = 2 * i + q
                dve.wait_ge(s_neighp[q], i + 1)
                if not isinstance(i, int) or i:
                    dve.wait_ge(s_out[q], 16 * i)
                dve.scalar_tensor_tensor(hbuf[:, q, 0, :], bank[3 + q][:, 0:D], invT[:, bass.ds(t, 1)],
                                         xr[:, bass.ds(t, 1), :].rearrange("p a d -> p (a d)"),
                                         ALU.mult, ALU.add).then_inc(s_res[q], 1)

            def two_tiles(i):
                result(i, 0)
                result(i, 1)

            two_tiles(0)
            loop(dve, two_tiles, 1, TF // 2)
            result(TF // 2, 0)


_INS = ["x", "src", "dst", "edge_attr_64", "L0_gnn_W1", "L0_gnn_b1", "L0_gnn_W2", "L0_gnn_b2",
        "L1_gnn_w_neigh", "L1_gnn_w_self", "L1_gnn_b_self"]
_TRANSPOSED = ("L1_gnn_w_neigh", "L1_gnn_w_self")


def kernel(**inputs):
    import numpy as _np
    import concourse.bacc as _bacc
    from concourse import mybir as _mybir
    from concourse.bass_utils import run_bass_kernel_spmd as _run

    nc = _bacc.Bacc("TRN2", target_bir_lowering=False, num_devices=1)
    arrays, args = {}, []
    for name in _INS:
        a = _np.asarray(inputs[name])
        a = _np.ascontiguousarray(a.T if name in _TRANSPOSED else a)
        arrays[f"in_{name}_dram"] = a
        args.append(nc.dram_tensor(f"in_{name}_dram", a.shape, _mybir.dt.from_np(a.dtype), kind="ExternalInput").ap())
    n, d = inputs["x"].shape
    out = nc.dram_tensor("out_dram", (n, d), _mybir.dt.float32, kind="ExternalOutput").ap()
    gnn_kernel(nc, *args, out)
    r = _run(nc, [arrays], core_ids=[0])
    return r.results[0]["out_dram"]
```

```python
from contextlib import ExitStack

import numpy as np

import concourse.bass as bass
from concourse import mybir
from concourse.alu_op_type import AluOpType as ALU

ACT = mybir.ActivationFunctionType
AX = mybir.AxisListType
F32 = mybir.dt.float32
F16 = mybir.dt.float16
BF16 = mybir.dt.bfloat16
I32 = mybir.dt.int32
U32 = mybir.dt.uint32

P = 128


def gnn_kernel(nc, x, src, dst, edges, w1, b1, w2, b2, wneighT, wselfT, bself, out):
    N, D = x.shape
    E, FE = edges.shape
    HID = w1.shape[1]
    DH = D // P
    HB = HID // P
    CH = 8
    GE = CH * P
    G = -(-E // GE)
    GF = G - 1
    REPEATED = GF * GE - (E - GE)
    G0 = min(G, P)
    G1 = G - G0
    T = 2 * (-(-N // (2 * P)))
    NP = T * P
    TF = N // P
    REST = N - TF * P
    TN = TF + 1
    U = T // 2
    WIN = 48
    NW = -(-N // WIN)
    PAIRS = G // 2
    NM = 2 * P
    SL = P
    CB = NP // 2 // P
    CT = P // 2
    KEYS = 2 * TN
    SC = 8
    ST = CT // SC
    BC = SC // 2
    KB = 5
    NOKEY = 1024.0
    SCALE = 2048.0
    EPS = 1e-5
    assert G % 2 == 0 and G1 < P and PAIRS > T and U % 2 == 1 and FE == 64 and NP >= N + WIN
    assert TN % 2 == 1 and T == TN + 1 and CB % KB == 0 and CB == U and BC * KEYS <= 512 and E < 2 ** 24

    ctx = ExitStack()
    with ctx:
        def sb(name, shape, dt):
            return ctx.enter_context(nc.sbuf_tensor(name, shape, dt))

        def sem(name):
            return ctx.enter_context(nc.semaphore(name))

        def sems(name):
            return [sem(f"{name}{q}") for q in range(2)]

        table = nc.dram_tensor("h1_table", (NP, 2 * D), F16).ap()

        xr = sb("xr", [P, T, D], F32)
        hreg = sb("hreg", [P, T, D], F32)
        h0T = hreg[:, :, :].rearrange("p t (h n) -> p t h n", h=DH)
        htab = hreg[:, :, :].rearrange("p t d -> p (t d)").bitcast(F16).rearrange("p (t d) -> p t d", t=T)
        sumT = hreg[:, :, :].rearrange("p t d -> p (t d)").rearrange("p (h n) -> p h n", h=DH)
        areg = sb("areg", [P, NP], F32)
        acc = areg
        adj = areg[:, :].bitcast(BF16)[:, 0:2 * P * TN].rearrange("p (q n h) -> p q n h", q=2, n=P)
        rs1 = sb("rs1", [P, T], F32)
        nm1 = sb("nm1", [P, T], F32)
        cntN = sb("cntN", [P, T], F32)
        invT = sb("invT", [P, T], F32)
        relT = sb("relT", [P, G, CH], F32)
        base = sb("base", [1, G], I32)
        flag = sb("flag", [1, 2], I32)
        kreg = sb("kreg", [P, 2, CB, SL], I32)
        pairs16 = kreg[:, :, :, :].rearrange("p k b s -> p (k b s)").bitcast(F16).rearrange(
            "p (k j d) -> p k j d", k=2, d=2)
        w1a = sb("w1a", [FE, HID], F32)
        w1b = sb("w1b", [P, DH, HID], F32)
        w2s = sb("w2s", [P, HB, D], F32)
        wns = sb("wns", [P, DH, D], F32)
        wss = sb("wss", [P, DH, D], F32)
        b1T = sb("b1T", [P, HB], F32)
        b2bc = sb("b2bc", [P, D], F32)
        bsbc = sb("bsbc", [P, D], F32)
        ident = sb("ident", [P, P], F32)
        ones = sb("ones", [P, P], F32)
        iota = sb("iota", [P, WIN], F32)
        iota16 = sb("iota16", [P, P], F16)
        below = sb("below", [P, 2, P], F32)
        tiles_before = sb("tiles_before", [T, CB], F32)
        node0 = sb("node0", [P, CB], F32)
        edg = sb("edg", [P, 2, CH, FE], F32)
        oneh = sb("oneh", [P, 2, CH, WIN], F32)
        hbuf = sb("hbuf", [P, 2, 2, D], F32)
        hids = sb("hids", [P, 2, HB, NM], F32)
        inv64 = sb("inv64", [FE, 2, NM], F32)
        aggn = sb("aggn", [FE, 2, NM], F32)
        st6 = sb("st6", [P, 2, 2, 6], F32)
        mv = sb("mv", [P, 2, 2, 2], F32)
        ve = sb("ve", [P, 2, 2], F32)
        sd = sb("sd", [P, 2, 2], F32)
        rsq = sb("rsq", [P, 2, 2], F32)
        nmq = sb("nmq", [P, 2, 2], F32)
        st0 = sb("st0", [P, T, 6], F32)
        ln0 = sb("ln0", [P, 6, T], F32)
        viol = sb("viol", [P, 8], F32)
        noplace = sb("noplace", [P, CB // KB], F32)
        wstart = sb("wstart", [P, 1], F32)
        relw = sb("relw", [P, CH], F32)
        tot = sb("tot", [T, 1], F32)
        totb = sb("totb", [T, CB], F32)
        startu = sb("startu", [P, CB], U32)
        kf = [edg[:, :, :, :].rearrange("p q c f -> p (q c f)")[:, 0:KB * SL],
              oneh[:, :, :, :].rearrange("p q c w -> p (q c w)")[:, 0:KB * SL],
              relT[:, :, :].rearrange("p g c -> p (g c)")[:, 0:KB * SL]]
        kf.append(relT[:, :, :].rearrange("p g c -> p (g c)")[:, KB * SL:2 * KB * SL])
        away = areg[:, 0:KB * SL]
        khi = areg[:, KB * SL:2 * KB * SL].bitcast(I32)
        h16 = hids[:, :, :, :].rearrange("p a b n -> p (a b n)").bitcast(BF16)
        onesrc = h16[:, 0:2 * SC * P].rearrange("p (q c n) -> p q c n", q=2, c=SC)
        onekey = h16[:, 2 * SC * P:2 * SC * (P + KEYS)].rearrange("p (q c k) -> p q c k", q=2, c=SC)
        layer1 = edg[:, :, :, :].rearrange("p q c f -> p (q c f)")
        sumN = layer1[:, 0:D]
        h1buf = layer1[:, D:2 * D]
        bothT = hbuf[:, 1, :, :].rearrange("p k d -> p (k d)")
        finished = [hbuf[:, 0, q, :] for q in range(2)]
        raw = kreg[:, :, :, :].rearrange("p k b s -> p (k b s)")[:, 0:4 * GE].bitcast(F32).rearrange(
            "p (k b j) -> p k b j", k=2, b=2)
        rawi = kreg[:, :, :, :].rearrange("p k b s -> p (k b s)")[:, 0:4 * GE].rearrange(
            "p (k b j) -> p k b j", k=2, b=2)
        relr = hids[:, :, :, :].rearrange("p a b n -> p (a b n)").rearrange("p (b j) -> p b j", b=2)
        dstT0 = kreg[:, :, :, :].rearrange("p k b s -> p (k b s)")[:, 4 * GE:4 * GE + G * CH].bitcast(F32).rearrange(
            "p (g c) -> p g c", c=CH)
        rows = kreg[:, :, :, :].rearrange("p k b s -> p (k b s)").bitcast(F16)[:, 0:CH * 2 * D].rearrange(
            "p (c d) -> p c d", c=CH)
        srcT = kreg[:, :, :, :].rearrange("p k b s -> p (k b s)")[:, 4 * GE:4 * GE + G * CH].bitcast(U32).rearrange(
            "p (g c) -> p g c", c=CH)
        raw1 = areg[:, 0:4 * GE].rearrange("p (k b j) -> p k b j", k=2, b=2)
        raw1i = areg[:, 0:4 * GE].bitcast(I32).rearrange("p (k b j) -> p k b j", k=2, b=2)
        dstT1 = areg[:, 4 * GE:4 * GE + G * CH].rearrange("p (g c) -> p g c", c=CH)
        oneb = oneh[:, :, :, :].rearrange("p q c w -> p (q c w)").bitcast(BF16)[:, 0:CH * WIN].rearrange(
            "p (c w) -> p c w", c=CH)
        stage = sb("stage", [P, CH], U32)

        cpl = [ctx.enter_context(nc.psum_tensor(f"couples{n}", [P, 2, 512], F32)) for n in range(2)]
        bank = [cpl[0][:, 0, :], cpl[0][:, 1, :], cpl[1][:, 0, :], cpl[1][:, 1, :]]
        bank += [ctx.enter_context(nc.psum_tensor(f"bank{n}", [P, 512], F32))[:, :] for n in range(4, 8)]

        s_raw = sem("s_raw")
        s_x = sem("s_x")
        s_w = sem("s_w")
        s_zero = sem("s_zero")
        s_const = sem("s_const")
        s_viol = sem("s_viol")
        s_violT = sem("s_violT")
        s_flag = sem("s_flag")
        s_rel = sem("s_rel")
        s_idx_tr = sem("s_idx_tr")
        s_idx_act = sem("s_idx_act")
        s_masked = sem("s_masked")
        s_var0 = sem("s_var0")
        s_sd0 = sem("s_sd0")
        s_ln0 = sem("s_ln0")
        s_h0 = sem("s_h0")
        s_h0tr = sem("s_h0tr")
        s_h0T = sem("s_h0T")
        s_b2 = sem("s_b2")
        s_edges = sems("s_edges_")
        s_oneh = sems("s_oneh_")
        s_esum = sems("s_esum_")
        s_added = sems("s_added_")
        s_acc = sem("s_acc")
        s_cntp = sem("s_cntp")
        s_cnt = sem("s_cnt")
        s_cntT = sem("s_cntT")
        s_totb = sem("s_totb")
        s_startp = sem("s_startp")
        s_start = sem("s_start")
        s_places = sem("s_places")
        s_keys = sem("s_keys")
        s_keytr = sem("s_keytr")
        s_keyT = sem("s_keyT")
        s_loT = sem("s_loT")
        s_nopl = sem("s_nopl")
        s_noplp = sem("s_noplp")
        s_flag1 = sem("s_flag1")
        s_agg = sems("s_agg_")
        s_hidp = sems("s_hidp_")
        s_hids = sems("s_hids_")
        s_outp = sems("s_outp_")
        s_x1 = sems("s_x1_")
        s_var1 = sems("s_var1_")
        s_sd1 = sems("s_sd1_")
        s_ln1 = sems("s_ln1_")
        s_hi = sems("s_hi_")
        s_tab = sems("s_tab_")
        s_one = sem("s_one")
        s_cplp = sem("s_cplp")
        s_adj = sem("s_adj")
        s_dense = sem("s_dense")
        s_sumN = sem("s_sumN")
        s_h1 = sem("s_h1")
        s_bs = sem("s_bs")
        s_trp = sem("s_trp")
        s_trs = sem("s_trs")
        s_outq = sem("s_outq")
        s_res = sem("s_res")
        s_out = sems("s_out_")
        a_tr = sem("a_tr")
        a_trc = sem("a_trc")
        a_edges = sem("a_edges")
        a_oneh = sem("a_oneh")
        a_sum = sem("a_sum")
        a_group = sem("a_group")
        n_raw = sem("n_raw")
        n_rawf = sem("n_rawf")
        n_tr = sem("n_tr")
        n_trc = sem("n_trc")
        n_table = sem("n_table")
        n_h = sem("n_h")
        n_hT = sem("n_hT")
        n_hTs = sem("n_hTs")
        n_selfp = sem("n_selfp")
        n_self = sem("n_self")
        n_stage = sem("n_stage")
        n_rows = sem("n_rows")
        n_oneb = sem("n_oneb")
        n_sum = sem("n_sum")
        n_group = sem("n_group")
        n_zero = sem("n_zero")
        n_done = sem("n_done")
        n_sumc = sem("n_sumc")
        n_neighp = sem("n_neighp")
        n_res = sem("n_res")
        n_out = sem("n_out")

        def edge_rows(g):
            return edges[bass.ds(g * GE, GE), :].rearrange("(p c) f -> p (c f)", c=CH)

        last_edge_rows = edges[E - GE:E, :].rearrange("(p c) f -> p (c f)", c=CH)

        def in_windows(eng):
            eng.wait_ge(s_flag, 1)
            return eng.value_load(flag[0:1, 0:1], min_val=0, max_val=1) < 1

        def in_places(eng):
            eng.wait_ge(s_flag1, 1)
            return eng.value_load(flag[0:1, 1:2], min_val=0, max_val=1) < 1

        def kslot(b):
            return 2 * (b // KB % 2)

        def later(i):
            return not isinstance(i, int) or i > 0

        def loop(eng, body, first, end, step=1):
            with eng.Fori(first, end, step) as i:
                body(i)

        def load_index_tables(sp, into, done, what):
            for k, v in what:
                sp.dma_start(into[0:G0, k, 0, :], v[0:G0 * GE].rearrange("(g j) -> g j", g=G0)).then_inc(done, 16)
                sp.dma_start(into[0:G1 - 1, k, 1, :],
                             v[G0 * GE:GF * GE].rearrange("(g j) -> g j", g=G1 - 1)).then_inc(done, 16)
                sp.dma_start(into[G1 - 1:G1, k, 1, :], v[E - GE:E].rearrange("(g j) -> g j", g=1)).then_inc(done, 16)

        def transpose_table(pe, into, tab, c):
            for b, m in ((0, G0), (1, G1)):
                ins = pe.transpose(into[:, b * P:b * P + m],
                                   tab[0:m, b, :].rearrange("g (p c) -> g c p", c=CH)[:, c, :], ident[0:m, 0:m])
            return ins

        def mask_repeated(pool, v):
            return pool.affine_select(out=v[:, GF, :], in_=v[:, GF, :], compare_op=ALU.is_ge, fill=-NOKEY * 8,
                                      base=-REPEATED, pattern=[[1, CH]], channel_multiplier=CH)

        def tile_of(v, t):
            return v[:, bass.ds(t, 1), :].rearrange("p a d -> p (a d)")

        block = ctx.enter_context(nc.Block())

        @block.sync
        def _(sp):
            load_index_tables(sp, rawi, s_raw, [(0, dst)])
            with nc.allow_non_contiguous_dma(reason="one index of each group"):
                sp.dma_start(base[0:1, 0:GF], dst[0:GF * GE].rearrange("(g j) -> j g", g=GF)[0:1, :]).then_inc(s_raw, 16)
            sp.dma_start(base[0:1, GF:G], dst[E - GE:E - GE + 1].rearrange("(a b) -> a b", a=1)).then_inc(s_raw, 16)
            sp.wait_ge(s_zero, 1)
            step = 8
            for t in range(0, TF, step):
                m = min(step, TF - t)
                sp.dma_start(xr[:, t:t + m, :], x[t * P:(t + m) * P, :].rearrange("(t p) d -> p t d", p=P)).then_inc(s_x, 16)
            sp.dma_start(xr[0:REST, TF, :], x[TF * P:N, :]).then_inc(s_x, 16)
            sp.dma_start(b2bc[:, :], b2.rearrange("(a n) -> a n", a=1).broadcast_to([P, D])).then_inc(s_w, 16)
            sp.dma_start(bsbc[:, :], bself.rearrange("(a n) -> a n", a=1).broadcast_to([P, D])).then_inc(s_w, 16)
            sp.dma_start(w1a[:, :], w1[0:FE, :]).then_inc(s_w, 16)
            sp.dma_start(w1b[:, :, :], w1[FE:FE + D, :].rearrange("(h p) n -> p h n", p=P)).then_inc(s_w, 16)
            sp.dma_start(w2s[:, :, :], w2.rearrange("(h p) n -> p h n", p=P)).then_inc(s_w, 16)
            sp.dma_start(wns[:, :, :], wneighT.rearrange("(h p) n -> p h n", p=P)).then_inc(s_w, 16)
            sp.dma_start(wss[:, :, :], wselfT.rearrange("(h p) n -> p h n", p=P)).then_inc(s_w, 16)
            with nc.allow_non_contiguous_dma(reason="a bias on the partitions"):
                sp.dma_start(b1T[:, :], b1.rearrange("(h p) -> p h", p=P)).then_inc(s_w, 16)

            with sp.If(in_windows(sp)):
                def load(i, q, rows_of=None):
                    if later(i):
                        sp.wait_ge(s_esum[q], i)
                    sp.dma_start(edg[:, q, :, :].rearrange("p c f -> p (c f)"),
                                 edge_rows(2 * i + q) if rows_of is None else rows_of).then_inc(s_edges[q], 16)

                def both(i):
                    load(i, 0)
                    load(i, 1)

                both(0)
                loop(sp, both, 1, PAIRS - 1)
                load(PAIRS - 1, 0)
                load(PAIRS - 1, 1, last_edge_rows)
            with sp.Else():
                def load_any(g, rows_of=None):
                    if later(g):
                        sp.wait_ge(a_group, g)
                    sp.dma_start(edg[:, 0, :, :].rearrange("p c f -> p (c f)"),
                                 edge_rows(g) if rows_of is None else rows_of).then_inc(a_edges, 16)

                load_any(0)
                loop(sp, load_any, 1, GF)
                load_any(GF, last_edge_rows)

            with sp.If(in_places(sp)):
                def result(i, q, n=P):
                    sp.wait_ge(s_res, 2 * i + q + 1)
                    sp.dma_start(out[bass.ds((2 * i + q) * P, n), :], finished[q][0:n, :]).then_inc(s_out[q], 16)

                def two(i):
                    result(i, 0)
                    result(i, 1)

                loop(sp, two, 0, TF // 2)
                result(TF // 2, 0, REST)
                sp.wait_ge(s_out[0], 16 * (TF // 2 + 1))
                sp.wait_ge(s_out[1], 16 * (TF // 2))
            with sp.Else():
                sp.wait_ge(s_tab[0], U // 2 + 1)
                sp.wait_ge(s_tab[1], U // 2)
                sp.dma_start(table.rearrange("(t p) d -> p t d", p=P), htab).then_inc(n_table, 16)
                load_index_tables(sp, raw1i, n_raw, [(0, dst), (1, src)])

                def any_result(t, n=P):
                    sp.wait_ge(n_res, t + 1)
                    sp.dma_start(out[bass.ds(t * P, n), :], hbuf[0:n, 0, 0, :]).then_inc(n_out, 16)

                loop(sp, any_result, 0, TF)
                any_result(TF, REST)
                sp.wait_ge(n_out, 16 * TN)

        @block.gpsimd
        def _(pool):
            pool.memset(xr[:, TF:T, :], 0.0).then_inc(s_zero, 1)
            pool.memset(viol[:, :], 0.0)
            pool.memset(ident[:, :], 0.0)
            pool.memset(ones[:, :], 1.0)
            pool.memset(below[:, :, :], 0.0)
            pool.memset(tiles_before[:, :], 0.0)
            pool.iota(iota[:, :], pattern=[[1, WIN]], base=0, channel_multiplier=0,
                      allow_small_or_imprecise_dtypes=True)
            pool.iota(iota16[:, :], pattern=[[1, P]], base=0, channel_multiplier=0,
                      allow_small_or_imprecise_dtypes=True)
            pool.iota(node0[:, :], pattern=[[2 * P, CB]], base=0, channel_multiplier=2,
                      allow_small_or_imprecise_dtypes=True)
            pool.drain()
            pool.affine_select(out=ident[:, :], in_=ident[:, :], compare_op=ALU.not_equal, fill=1.0,
                               base=0, pattern=[[-1, P]], channel_multiplier=1)
            for k in range(2):
                pool.affine_select(out=below[:, k, :], in_=below[:, k, :], compare_op=ALU.is_ge, fill=1.0,
                                   base=k * P, pattern=[[-2, P]], channel_multiplier=1)
            pool.affine_select(out=tiles_before[:, :], in_=tiles_before[:, :], compare_op=ALU.is_ge, fill=1.0,
                               base=0, pattern=[[-2, CB]], channel_multiplier=1).then_inc(s_const, 1)
            pool.memset(acc[:, :], 0.0).then_inc(s_const, 1)
            pool.wait_ge(s_idx_act, CH)
            mask_repeated(pool, relT).then_inc(s_masked, 1)

            pool.wait_ge(s_w, 8 * 16)

            def add_b2(u):
                pool.wait_ge(s_h0, 2 * u + 2)
                v = xr[:, bass.ds(2 * u, 2), :]
                pool.tensor_tensor(v, v, b2bc[:, :].unsqueeze(1).broadcast_to([P, 2, D]), ALU.add).then_inc(s_b2, 1)

            loop(pool, add_b2, 0, U)

            with pool.If(in_windows(pool)):
                pool.nop()
            with pool.Else():
                pool.wait_ge(a_trc, CH)
                mask_repeated(pool, dstT0).then_inc(s_masked, 1)

            pool.wait_ge(s_start, 1)
            for b in range(CB):
                for k, v in enumerate((dst, src)):
                    pool.indirect_dma_start(kreg[:, k, b, :], None, v.rearrange("(e a) -> e a", a=1),
                                            bass.IndirectOffsetOnAxis(ap=startu[:, b:b + 1], axis=0)).then_inc(s_places, 16)

            with pool.If(in_places(pool)):
                def add_bs(t):
                    pool.wait_ge(s_h1, t + 1)
                    v = tile_of(xr, t)
                    pool.tensor_tensor(v, v, bsbc[:, :], ALU.add).then_inc(s_bs, 1)

                loop(pool, add_bs, 0, TN)
            with pool.Else():
                pool.wait_ge(n_trc, 2 * CH)
                mask_repeated(pool, dstT1).then_inc(s_masked, 2)

                def any_group(n):
                    pool.wait_ge(n_table, 16)
                    pool.wait_ge(n_stage, n)
                    for c in range(CH):
                        pool.indirect_dma_start(rows[:, c, :], None, table,
                                                bass.IndirectOffsetOnAxis(ap=stage[:, c:c + 1], axis=0)).then_inc(n_rows, 16)

                loop(pool, any_group, 1, G + 1)

        @block.scalar
        def _(act):
            for c in range(CH):
                act.wait_ge(s_idx_tr, c + 1)
                act.activation(relT[:, :, c], bank[c % 2][:, 0:G], ACT.Copy).then_inc(s_idx_act, 1)
            act.wait_ge(s_var0, 1)
            act.activation(ln0[:, 3, :], ln0[:, 1, :], ACT.Sqrt).then_inc(s_sd0, 1)
            act.wait_ge(s_ln0, 1)

            def h0(u):
                if later(u):
                    act.wait_ge(s_h0tr, u)
                for t in range(2):
                    act.activation(hbuf[:, 0, t, :], tile_of(xr, 2 * u + t), ACT.Relu, bias=ln0[:, 5, bass.ds(2 * u + t, 1)],
                                   scale=ln0[:, 4, bass.ds(2 * u + t, 1)]).then_inc(s_h0, 1)
                act.wait_ge(s_h0tr, u + 1)
                act.activation(h0T[:, bass.ds(2 * u, 2), :, :],
                               bank[4][:, :].rearrange("p (t h n) -> p t h n", t=2, h=DH), ACT.Copy).then_inc(s_h0T, 1)

            h0(0)
            loop(act, h0, 1, U)

            with act.If(in_windows(act)):
                act.nop()
            with act.Else():
                for c in range(CH):
                    act.wait_ge(a_tr, c + 1)
                    act.activation(dstT0[:, :, c], bank[c % 2][:, 0:G], ACT.Copy).then_inc(a_trc, 1)

            def hidden(i, q):
                if later(i):
                    act.wait_ge(s_outp[q], i)
                for k in range(2):
                    act.wait_ge(s_hidp[q], 2 * i + k + 1)
                    for b in range(2):
                        ins = act.activation(hids[:, q, 2 * k + b, :], bank[2 + 2 * q + k][:, b * NM:(b + 1) * NM],
                                             ACT.Relu, bias=b1T[:, 2 * k + b:2 * k + b + 1])
                    ins.then_inc(s_hids[q], 1)

            def sd_of(i, q):
                act.wait_ge(s_var1[q], i + 1)
                act.activation(sd[:, q, :], ve[:, q, :], ACT.Sqrt).then_inc(s_sd1[q], 1)

            def h1(i, q):
                u = 2 * i + q
                act.wait_ge(s_ln1[q], i + 1)
                if later(i):
                    act.wait_ge(s_tab[q], i)
                for t in range(2):
                    act.activation(hbuf[:, q, t, :], tile_of(xr, 2 * u + t),
                                   ACT.Relu, bias=nmq[:, q, t:t + 1], scale=rsq[:, q, t:t + 1])
                act.drain()
                act.activation(htab[:, bass.ds(2 * u, 2), 0:D], hbuf[:, q, :, :], ACT.Copy).then_inc(s_hi[q], 1)

            def layer0(i):
                hidden(i, 0)
                hidden(i, 1)
                for q in range(2):
                    sd_of(i, q)
                for q in range(2):
                    h1(i, q)

            layer0(0)
            loop(act, layer0, 1, U // 2)
            hidden(U // 2, 0)
            sd_of(U // 2, 0)
            h1(U // 2, 0)
            act.wait_ge(s_tab[0], U // 2 + 1)
            act.wait_ge(s_tab[1], U // 2)

            for b in range(CB):
                act.wait_ge(s_keytr, 2 * b + 2)
                act.activation(pairs16[:, 1, b * P:(b + 1) * P, :],
                               bank[2 + b % 2][:, 0:P].unsqueeze(2).broadcast_to([P, P, 2]), ACT.Copy).then_inc(s_loT, 1)

            def copy_counts(t, par, s):
                act.wait_ge(s_cplp, t * ST + s + 1)
                act.activation(adj[:, par, :, :].rearrange("p n h -> p (n h)")[:, s * SC * KEYS:(s + 1) * SC * KEYS].rearrange("p (a k) -> p a k", a=2),
                               cpl[s % 2][:, :, 0:BC * KEYS], ACT.Copy).then_inc(s_adj, 1)

            def h1_tile(t):
                if later(t):
                    act.wait_ge(s_trp, t)
                act.activation(h1buf[:, :], tile_of(xr, t), ACT.Relu,
                               bias=nm1[:, bass.ds(t, 1)], scale=rs1[:, bass.ds(t, 1)]).then_inc(s_h1, 1)

            def copy_transposed(t):
                act.wait_ge(s_trp, t + 1)
                if later(t):
                    act.wait_ge(s_outq, t)
                act.activation(bothT, bank[6][:, :], ACT.Copy).then_inc(s_trs, 1)

            with act.If(in_places(act)):
                def tile(t, par, first=False, last=False):
                    if not first and not last:
                        act.wait_ge(s_dense, t)
                    for s in range(ST):
                        if not last:
                            copy_counts(t + 1, 1 - par, s)
                        if s == 1 and not first:
                            h1_tile(t - 1)
                        if s == 3 and not first:
                            copy_transposed(t - 1)

                for s in range(ST):
                    copy_counts(0, 0, s)
                tile(0, 0, first=True)
                tile(1, 1)
                tile(2, 0)
                with act.Fori(1, TN // 2 - 1) as i:
                    tile(2 * i + 1, 1)
                    tile(2 * i + 2, 0)
                tile(TN - 2, 1)
                tile(TN - 1, 0, last=True)
                h1_tile(TN - 1)
                copy_transposed(TN - 1)
            with act.Else():
                for c in range(CH):
                    for k in range(2):
                        act.wait_ge(n_tr, 2 * c + k + 1)
                        act.activation((dstT1, srcT)[k][:, :, c], bank[2 * k + c % 2][:, 0:G], ACT.Copy).then_inc(n_trc, 1)

                def self_part(t):
                    if later(t):
                        act.wait_ge(n_hT, t)
                    act.activation(hbuf[:, 0, 0, :], tile_of(xr, t), ACT.Relu,
                                   bias=nm1[:, bass.ds(t, 1)], scale=rs1[:, bass.ds(t, 1)]).then_inc(n_h, 1)
                    act.wait_ge(n_hT, t + 1)
                    if later(t):
                        act.wait_ge(n_selfp, t)
                    act.activation(hbuf[:, 0, 1, :], bank[4][:, 0:D], ACT.Copy).then_inc(n_hTs, 1)

                self_part(0)
                loop(act, self_part, 1, TN)

                def any_src(g):
                    if later(g):
                        act.wait_ge(n_group, g)
                    act.activation(stage[:, :], tile_of(srcT, g), ACT.Copy).then_inc(n_stage, 1)

                any_src(0)
                loop(act, any_src, 1, G)

                act.wait_ge(n_done, 1)

                def copy_sums(t):
                    if later(t):
                        act.wait_ge(n_neighp, t)
                    act.activation(hids[:, 0, 0, :].rearrange("p (h n) -> p h n", h=DH),
                                   sumT[:, :, bass.ds(t * P, P)], ACT.Copy).then_inc(n_sumc, 1)

                copy_sums(0)
                loop(act, copy_sums, 1, TN)

        @block.tensor
        def _(pe):
            pe.wait_ge(s_const, 1)
            pe.wait_ge(s_rel, 1)
            for c in range(CH):
                if c >= 2:
                    pe.wait_ge(s_idx_act, c - 1)
                transpose_table(pe, bank[c % 2], relr, c).then_inc(s_idx_tr, 1)
            pe.wait_ge(s_viol, 1)
            pe.transpose(bank[7][0:1, 0:P], viol[:, 0:1], ident[:, :]).then_inc(s_violT, 1)

            def h0tr(u):
                pe.wait_ge(s_h0, 2 * u + 2)
                if later(u):
                    pe.wait_ge(s_h0T, u)
                for t in range(2):
                    for h in range(DH):
                        ins = pe.transpose(bank[4][:, (t * DH + h) * P:(t * DH + h + 1) * P],
                                           hbuf[:, 0, t, h * P:(h + 1) * P], ident[:, :])
                ins.then_inc(s_h0tr, 1)

            def edge_sums(into, q):
                for c in range(CH):
                    pe.matmul(into[0:FE, 0:WIN], edg[:, q, c, :], oneh[:, q, c, :], start=(c == 0), stop=(c == CH - 1))
                for c in range(CH):
                    ins = pe.matmul(into[FE:P, 0:WIN], ones[:, 0:FE], oneh[:, q, c, :], start=(c == 0), stop=(c == CH - 1))
                return ins

            with pe.If(in_windows(pe)):
                def group(i, q):
                    pe.wait_ge(s_edges[q], 16 * (i + 1))
                    pe.wait_ge(s_oneh[q], i + 1)
                    if later(i):
                        pe.wait_ge(s_added[q], i)
                    else:
                        pe.wait_ge(s_idx_act, CH)
                    edge_sums(bank[q], q).then_inc(s_esum[q], 1)

                def with_h0(i):
                    group(i, 0)
                    h0tr(i)
                    group(i, 1)

                def groups(i):
                    group(i, 0)
                    group(i, 1)

                with_h0(0)
                loop(pe, with_h0, 1, U)
                loop(pe, groups, U, PAIRS)
            with pe.Else():
                h0tr(0)
                loop(pe, h0tr, 1, U)
                for c in range(CH):
                    if c >= 2:
                        pe.wait_ge(a_trc, c - 1)
                    transpose_table(pe, bank[c % 2], raw[:, 0], c).then_inc(a_tr, 1)
                pe.wait_ge(a_trc, CH)

                def any_group(g):
                    with pe.Fori(0, NW) as w:
                        pe.wait_ge(a_edges, 16 * (g + 1))
                        pe.wait_ge(a_oneh, g * NW + w + 1)
                        edge_sums(bank[0], 0).then_inc(a_sum, 1)

                loop(pe, any_group, 0, G)

            pe.wait_ge(s_acc, 1)
            for t in range(T):
                ins = pe.matmul(bank[0][:, t:t + 1], acc[FE:FE + 1, t * P:(t + 1) * P], ones[FE:FE + 1, 0:1],
                                start=True, stop=True)
            ins.then_inc(s_cntp, 1)
            pe.wait_ge(s_cnt, 1)
            pe.transpose(bank[1][0:T, 0:P], cntN[:, :], ident[:, :]).then_inc(s_cntT, 1)
            for k in range(2):
                pe.matmul(bank[0][:, 0:CB], below[:, k, :], cntN[:, :].rearrange("p (b k) -> p k b", k=2)[:, k, :],
                          start=(k == 0), stop=False)
            pe.wait_ge(s_totb, 1)
            pe.matmul(bank[0][:, 0:CB], ones[0:T, :], totb[:, :], start=False, stop=True).then_inc(s_startp, 1)

            pe.wait_ge(s_w, 8 * 16)
            pe.wait_ge(s_h0T, U)

            def hidden(i, q):
                u = 2 * i + q
                pe.wait_ge(s_agg[q], i + 1)
                for k in range(2):
                    if later(i):
                        pe.wait_ge(s_hids[q], 2 * i + (k - 1))
                    for b in range(2):
                        o = bank[2 + 2 * q + k][:, b * NM:(b + 1) * NM]
                        cols = slice((2 * k + b) * P, (2 * k + b + 1) * P)
                        pe.matmul(o, w1a[:, cols], aggn[:, q, :], start=True, stop=False)
                        for h in range(DH):
                            ins = pe.matmul(o, w1b[:, h, cols], h0T[:, bass.ds(2 * u, 2), h, :], start=False, stop=(h == DH - 1))
                    ins.then_inc(s_hidp[q], 1)

            def outer(i, q):
                if later(i):
                    pe.wait_ge(s_x1[q], i)
                pe.wait_ge(s_hids[q], 2 * i + 2)
                for t in range(2):
                    for b in range(HB):
                        ins = pe.matmul(bank[6 + q][:, t * D:(t + 1) * D], hids[:, q, b, t * P:(t + 1) * P], w2s[:, b, :],
                                        start=(b == 0), stop=(b == HB - 1))
                ins.then_inc(s_outp[q], 1)

            def layer0(i):
                hidden(i, 0)
                hidden(i, 1)
                outer(i, 0)
                outer(i, 1)

            layer0(0)
            loop(pe, layer0, 1, U // 2)
            hidden(U // 2, 0)
            outer(U // 2, 0)
            pe.wait_ge(s_x1[0], U // 2 + 1)
            pe.wait_ge(s_x1[1], U // 2)
            pe.wait_ge(s_hids[0], 2 * (U // 2) + 2)

            for b in range(CB):
                if b % KB == 0:
                    pe.wait_ge(s_keys, b // KB + 1)
                if b >= 2:
                    pe.wait_ge(s_keyT, b - 1)
                    pe.wait_ge(s_loT, b - 1)
                j = b % KB
                pe.transpose(bank[b % 2][:, 0:P], kf[kslot(b)][:, j * SL:(j + 1) * SL], ident[:, :]).then_inc(s_keytr, 1)
                pe.transpose(bank[2 + b % 2][:, 0:P], kf[kslot(b) + 1][:, j * SL:(j + 1) * SL], ident[:, :]).then_inc(s_keytr, 1)
            pe.wait_ge(s_nopl, 1)
            pe.matmul(bank[7][0:1, 0:CB // KB], ones[:, 0:1], noplace[:, :], start=True, stop=True).then_inc(s_noplp, 1)

            def couples(t, s):
                n = t * ST + s
                pe.wait_ge(s_one, n + 1)
                if isinstance(n, int) and n < 2:
                    pe.wait_ge(s_keyT, CB)
                    pe.wait_ge(s_loT, CB)
                else:
                    pe.wait_ge(s_adj, n - 1)
                q = s % 2
                for c in range(SC):
                    ins = pe.matmul(cpl[q][:, c // BC, (c % BC) * KEYS:(c % BC + 1) * KEYS], onesrc[:, q, c, :],
                                    onekey[:, q, c, :], start=True, stop=True)
                ins.then_inc(s_cplp, 1)

            def dense(t, par, h0_, h1_):
                for h in range(h0_, h1_):
                    ins = pe.matmul(bank[4 + par], adj[:, par, :, h], htab[:, h, :], start=(h == 0), stop=(h == TN - 1))
                return ins

            def transposes(t):
                pe.wait_ge(s_sumN, t + 1)
                pe.wait_ge(s_h1, t + 1)
                if later(t):
                    pe.wait_ge(s_trs, t)
                for k, v in enumerate((sumN, h1buf)):
                    for h in range(DH):
                        ins = pe.transpose(bank[6][:, (2 * k + h) * P:(2 * k + h + 1) * P], v[:, h * P:(h + 1) * P], ident[:, :])
                ins.then_inc(s_trp, 1)

            def products(t):
                pe.wait_ge(s_trs, t + 1)
                if later(t):
                    pe.wait_ge(s_res, t)
                for k, w in enumerate((wns, wss)):
                    for h in range(DH):
                        ins = pe.matmul(bank[7][:, k * D:(k + 1) * D], bothT[:, (2 * k + h) * P:(2 * k + h + 1) * P],
                                        w[:, h, :], start=(h == 0), stop=(h == DH - 1))
                ins.then_inc(s_outq, 1)

            with pe.If(in_places(pe)):
                cut = [TN * s // ST for s in range(ST + 1)]

                def tile(t, par, first=False, last=False):
                    pe.wait_ge(s_adj, t * ST + ST)
                    if not first and not (isinstance(t, int) and t == 1):
                        pe.wait_ge(s_sumN, t - 1)
                    for s in range(ST):
                        if not last:
                            couples(t + 1, s)
                        ins = dense(t, par, cut[s], cut[s + 1])
                        if s == 2 and not first:
                            transposes(t - 1)
                        if s == 4 and not first:
                            products(t - 1)
                    ins.then_inc(s_dense, 1)

                for s in range(ST):
                    couples(0, s)
                tile(0, 0, first=True)
                tile(1, 1)
                tile(2, 0)
                with pe.Fori(1, TN // 2 - 1) as i:
                    tile(2 * i + 1, 1)
                    tile(2 * i + 2, 0)
                tile(TN - 2, 1)
                tile(TN - 1, 0, last=True)
                transposes(TN - 1)
                products(TN - 1)
            with pe.Else():
                for c in range(CH):
                    for k in range(2):
                        if c == 0:
                            pe.wait_ge(n_rawf, 1)
                        if c >= 2:
                            pe.wait_ge(n_trc, 2 * (c - 2) + k + 1)
                        transpose_table(pe, bank[2 * k + c % 2], raw1[:, k], c).then_inc(n_tr, 1)

                def self_part(t):
                    pe.wait_ge(n_h, t + 1)
                    if later(t):
                        pe.wait_ge(n_hTs, t)
                    for h in range(DH):
                        ins = pe.transpose(bank[4][:, h * P:(h + 1) * P], hbuf[:, 0, 0, h * P:(h + 1) * P], ident[:, :])
                    ins.then_inc(n_hT, 1)
                    pe.wait_ge(n_hTs, t + 1)
                    if later(t):
                        pe.wait_ge(n_self, t)
                    for h in range(DH):
                        ins = pe.matmul(bank[5][:, 0:D], hbuf[:, 0, 1, h * P:(h + 1) * P], wss[:, h, :],
                                        start=(h == 0), stop=(h == DH - 1))
                    ins.then_inc(n_selfp, 1)

                self_part(0)
                loop(pe, self_part, 1, TN)
                pe.wait_ge(n_trc, 2 * CH)

                def any_sums(g):
                    with pe.Fori(0, NW) as w:
                        pe.wait_ge(n_rows, 16 * CH * (g + 1))
                        pe.wait_ge(n_oneb, g * NW + w + 1)
                        for h in range(DH):
                            for c in range(CH):
                                for k in range(2):
                                    ins = pe.matmul(bank[0][:, h * WIN:(h + 1) * WIN],
                                                    rows[:, c, k * D + h * P:k * D + (h + 1) * P], oneb[:, c, :],
                                                    start=(c == 0 and k == 0), stop=(c == CH - 1 and k == 1))
                        ins.then_inc(n_sum, 1)

                loop(pe, any_sums, 0, G)

                def neigh(t):
                    pe.wait_ge(n_sumc, t + 1)
                    if later(t):
                        pe.wait_ge(n_res, t)
                    for h in range(DH):
                        ins = pe.matmul(bank[6][:, 0:D], hids[:, 0, 0, h * P:(h + 1) * P], wns[:, h, :],
                                        start=(h == 0), stop=(h == DH - 1))
                    ins.then_inc(n_neighp, 1)

                neigh(0)
                loop(pe, neigh, 1, TN)

        @block.vector
        def _(dve):
            dve.wait_ge(s_raw, 5 * 16)
            for b, m in ((0, G0), (1, G1)):
                dve.tensor_copy(raw[0:m, 0, b, :], rawi[0:m, 0, b, :])
            dve.drain()
            for b, m in ((0, G0), (1, G1)):
                ins = dve.tensor_scalar(relr[0:m, b, :], raw[0:m, 0, b, :], raw[0:m, 0, b, 0:1], None, ALU.subtract)
            ins.then_inc(s_rel, 1)
            dve.wait_ge(s_const, 1)
            dve.drain()
            for b, m in ((0, G0), (1, G1)):
                dve.tensor_reduce(viol[0:m, 2 * b + 1:2 * b + 2], relr[0:m, b, :], AX.X, ALU.max)
                dve.tensor_reduce(viol[0:m, 2 * b + 2:2 * b + 3], relr[0:m, b, :], AX.X, ALU.min)
            dve.drain()
            dve.tensor_scalar(viol[:, 5:6], viol[:, 1:2], viol[:, 3:4], float(WIN - 1), ALU.max, ALU.subtract)
            dve.tensor_scalar(viol[:, 6:7], viol[:, 2:3], viol[:, 4:5], -1.0, ALU.min, ALU.mult)
            dve.drain()
            dve.tensor_tensor(viol[:, 0:1], viol[:, 5:6], viol[:, 6:7], ALU.max).then_inc(s_viol, 1)
            dve.wait_ge(s_violT, 1)
            dve.tensor_reduce(viol[0:1, 7:8], bank[7][0:1, 0:P], AX.X, ALU.max)
            dve.drain()
            dve.tensor_scalar(flag[0:1, 0:1], viol[0:1, 7:8], 0.0, 1.0, ALU.max, ALU.min).then_inc(s_flag, 1)

            dve.wait_ge(s_x, 16 * (-(-TF // 8) + 1))
            with dve.Fori(0, T) as t:
                dve.bn_stats(tile_of(st0, t), tile_of(xr, t))
            dve.drain()
            mean, var, diff, root, rstd, nmr = (ln0[:, k, :] for k in range(6))
            dve.tensor_tensor(mean, st0[:, :, 1], st0[:, :, 4], ALU.add)
            dve.tensor_tensor(diff, st0[:, :, 1], st0[:, :, 4], ALU.subtract)
            dve.tensor_tensor(var, st0[:, :, 2], st0[:, :, 5], ALU.add)
            dve.drain()
            dve.tensor_tensor(diff, diff, diff, ALU.mult)
            dve.tensor_scalar(var, var, 1.0 / D, EPS, ALU.mult, ALU.add)
            dve.drain()
            dve.scalar_tensor_tensor(var, diff, 0.25, var, ALU.mult, ALU.add).then_inc(s_var0, 1)
            dve.wait_ge(s_sd0, 1)
            dve.reciprocal(rstd, root)
            dve.drain()
            dve.scalar_tensor_tensor(nmr, mean, -0.5, rstd, ALU.mult, ALU.mult).then_inc(s_ln0, 1)

            def add_window(into, start, part):
                v = into[..., bass.ds(start, WIN)]
                return dve.tensor_tensor(v, v, part, ALU.add)

            def in_window(o, rel):
                return dve.tensor_tensor(o, iota[:, :].unsqueeze(1).broadcast_to([P, CH, WIN]),
                                         rel.unsqueeze(2).broadcast_to([P, CH, WIN]), ALU.is_equal)

            dve.wait_ge(s_const, 2)
            dve.wait_ge(s_masked, 1)
            with dve.If(in_windows(dve)):
                def one_hot(i, q):
                    in_window(oneh[:, q, :, :], tile_of(relT, 2 * i + q)).then_inc(s_oneh[q], 1)

                def add(i, q):
                    start = dve.value_load(base[0:1, bass.ds(2 * i + q, 1)], min_val=0, max_val=N - 1)
                    dve.wait_ge(s_esum[q], i + 1)
                    if q == 1:
                        dve.wait_ge(s_added[0], i + 1)
                    elif later(i):
                        dve.wait_ge(s_added[1], i)
                    add_window(acc[:, :], start, bank[q][:, 0:WIN]).then_inc(s_added[q], 1)

                def both(i):
                    for q in range(2):
                        add(i, q)
                        one_hot(i + 1, q)

                one_hot(0, 0)
                one_hot(0, 1)
                both(0)
                loop(dve, both, 1, PAIRS - 1)
                add(PAIRS - 1, 0)
                add(PAIRS - 1, 1)
            with dve.Else():
                dve.wait_ge(s_masked, 2)
                with dve.Fori(0, G) as g:
                    dve.memset(wstart[:, :], 0.0)
                    dve.drain()
                    with dve.Fori(0, NW) as w:
                        dve.tensor_scalar(relw[:, :], tile_of(dstT0, g), wstart[:, 0:1], None, ALU.subtract)
                        dve.drain()
                        dve.tensor_scalar(wstart[:, :], wstart[:, :], float(WIN), None, ALU.add)
                        in_window(oneh[:, 0, :, :], relw[:, :]).then_inc(a_oneh, 1)
                        dve.wait_ge(a_sum, g * NW + w + 1)
                        add_window(acc[:, :], w * WIN, bank[0][:, 0:WIN])
                        dve.drain()
                    dve.nop().then_inc(a_group, 1)
            dve.drain()
            dve.nop().then_inc(s_acc, 1)

            dve.wait_ge(s_cntp, 1)
            dve.tensor_copy(cntN[:, :], bank[0][:, 0:T]).then_inc(s_cnt, 1)
            dve.wait_ge(s_cntT, 1)
            dve.tensor_reduce(tot[:, :], bank[1][0:T, 0:P], AX.X, ALU.add)
            dve.drain()
            dve.tensor_scalar(totb[:, :], tiles_before[:, :], tot[:, 0:1], None, ALU.mult).then_inc(s_totb, 1)
            dve.tensor_scalar(invT[:, :], cntN[:, :], 1.0, None, ALU.max)
            dve.wait_ge(s_startp, 1)
            dve.tensor_scalar(startu[:, :], bank[0][:, 0:CB], float(E - SL), None, ALU.min).then_inc(s_start, 1)
            dve.drain()
            dve.reciprocal(invT[:, :], invT[:, :])
            dve.tensor_scalar(acc[FE:P, :], acc[FE:P, :], 1.0, None, ALU.max)
            dve.drain()
            dve.tensor_scalar(invT[:, :], invT[:, :], 1.0 / SCALE, None, ALU.mult)
            dve.reciprocal(acc[FE:P, :], acc[FE:P, :])
            dve.drain()

            def mean_edges(i, q):
                u = 2 * i + q
                dve.tensor_copy(inv64[:, q, :], acc[FE:P, bass.ds(u * NM, NM)])
                dve.drain()
                dve.tensor_tensor(aggn[:, q, :], acc[0:FE, bass.ds(u * NM, NM)], inv64[:, q, :], ALU.mult).then_inc(s_agg[q], 1)

            def x1_stats(i, q):
                u = 2 * i + q
                v = xr[:, bass.ds(2 * u, 2), :]
                dve.wait_ge(s_outp[q], i + 1)
                dve.tensor_tensor(v, v, bank[6 + q][:, :].rearrange("p (t d) -> p t d", t=2), ALU.add).then_inc(s_x1[q], 1)
                dve.drain()
                for t in range(2):
                    dve.bn_stats(st6[:, q, t, :], tile_of(xr, 2 * u + t))
                dve.drain()
                for t in range(2):
                    dve.bn_aggr(mv[:, q, t, :], st6[:, q, t, :])
                dve.drain()
                dve.tensor_scalar(ve[:, q, :], mv[:, q, :, 1], EPS, None, ALU.add).then_inc(s_var1[q], 1)

            def ln1(i, q):
                u = 2 * i + q
                dve.wait_ge(s_sd1[q], i + 1)
                dve.reciprocal(sd[:, q, :], sd[:, q, :])
                dve.drain()
                dve.tensor_scalar(rsq[:, q, :], sd[:, q, :], SCALE, None, ALU.mult)
                dve.scalar_tensor_tensor(nmq[:, q, :], mv[:, q, :, 0], -SCALE, sd[:, q, :], ALU.mult, ALU.mult).then_inc(s_ln1[q], 1)
                dve.drain()
                dve.tensor_copy(rs1[:, bass.ds(2 * u, 2)], rsq[:, q, :])
                dve.tensor_copy(nm1[:, bass.ds(2 * u, 2)], nmq[:, q, :])

            def low_part(i, q):
                u = 2 * i + q
                dve.wait_ge(s_hi[q], i + 1)
                dve.tensor_tensor(htab[:, bass.ds(2 * u, 2), D:2 * D], hbuf[:, q, :, :], htab[:, bass.ds(2 * u, 2), 0:D],
                                  ALU.subtract).then_inc(s_tab[q], 1)

            dve.wait_ge(s_b2, U)
            mean_edges(0, 0)
            mean_edges(0, 1)

            def layer0(i, last=False):
                x1_stats(i, 0)
                mean_edges(i + 1, 0)
                if not last:
                    mean_edges(i + 1, 1)
                x1_stats(i, 1)
                ln1(i, 0)
                ln1(i, 1)
                low_part(i, 0)
                low_part(i, 1)

            loop(dve, layer0, 0, U // 2 - 1)
            layer0(U // 2 - 1, last=True)
            x1_stats(U // 2, 0)
            ln1(U // 2, 0)
            low_part(U // 2, 0)

            dve.wait_ge(s_places, 2 * CB * 16)
            for n in range(CB // KB):
                key, lo = kf[kslot(n * KB)], kf[kslot(n * KB) + 1]
                blocks = slice(n * KB, (n + 1) * KB)
                if n >= 2:
                    dve.wait_ge(s_keytr, 2 * KB * (n - 1))
                for b in range(KB):
                    dve.tensor_scalar(key[:, b * SL:(b + 1) * SL], kreg[:, 0, n * KB + b, :],
                                      node0[:, n * KB + b:n * KB + b + 1], None, ALU.subtract)
                dve.tensor_scalar(khi[:, :], kreg[:, 1, blocks, :].rearrange("p b s -> p (b s)"), 7, None, ALU.arith_shift_right)
                dve.drain()
                dve.scalar_tensor_tensor(away[:, :], key, -1.0, key, ALU.add, ALU.mult)
                dve.scalar_tensor_tensor(lo, khi[:, :], -float(P), kreg[:, 1, blocks, :].rearrange("p b s -> p (b s)"),
                                         ALU.mult, ALU.add)
                dve.scalar_tensor_tensor(key, key, float(TN), khi[:, :], ALU.mult, ALU.add)
                dve.drain()
                dve.tensor_scalar(away[:, :], away[:, :], 0.5, NOKEY, ALU.is_gt, ALU.mult)
                dve.drain()
                dve.tensor_reduce(noplace[:, n:n + 1], away[:, :], AX.X, ALU.add)
                dve.tensor_tensor(key, key, away[:, :], ALU.max).then_inc(s_keys, 1)
                for b in range(n * KB, (n + 1) * KB):
                    dve.wait_ge(s_keytr, 2 * b + 1)
                    dve.tensor_scalar(pairs16[:, 0, b * P:(b + 1) * P, :],
                                      bank[b % 2][:, 0:P].unsqueeze(2).broadcast_to([P, P, 2]), NOKEY, None,
                                      ALU.min).then_inc(s_keyT, 1)
            dve.drain()
            dve.nop().then_inc(s_nopl, 1)
            dve.wait_ge(s_noplp, 1)
            dve.tensor_reduce(viol[0:1, 1:2], bank[7][0:1, 0:CB // KB], AX.X, ALU.add)
            dve.drain()
            dve.tensor_scalar(flag[0:1, 1:2], viol[0:1, 1:2], NOKEY * (CB * P * SL - E), 1.0, ALU.not_equal,
                              ALU.mult).then_inc(s_flag1, 1)

            with dve.If(in_places(dve)):
                dve.wait_ge(s_loT, CB)

                def twice(n, k):
                    return pairs16[:, k, bass.ds(n * SC, SC), :]

                def one_hots(t, s):
                    n = t * ST + s
                    q = s % 2
                    if not isinstance(n, int) or n >= 2:
                        dve.wait_ge(s_cplp, n - 1)
                    for o, k, size in ((onesrc, 1, P), (onekey, 0, KEYS)):
                        ins = dve.tensor_tensor(o[:, q, :, :].rearrange("p c (v d) -> p c v d", d=2),
                                                iota16[:, 0:size].rearrange("p (v d) -> p v d", d=2).unsqueeze(1)
                                                .broadcast_to([P, SC, size // 2, 2]),
                                                twice(n, k).unsqueeze(2).broadcast_to([P, SC, size // 2, 2]), ALU.is_equal)
                    ins.then_inc(s_one, 1)

                def sum_parts(t, par):
                    dve.wait_ge(s_dense, t + 1)
                    if later(t):
                        dve.wait_ge(s_trp, t)
                    dve.tensor_copy(sumN[:, :], bank[4 + par][:, 0:D])
                    dve.drain()
                    dve.tensor_tensor(sumN[:, :], sumN[:, :], bank[4 + par][:, D:2 * D], ALU.add).then_inc(s_sumN, 1)

                def result(t, i, q):
                    dve.wait_ge(s_outq, t + 1)
                    dve.wait_ge(s_bs, t + 1)
                    if later(i):
                        dve.wait_ge(s_out[q], 16 * i)
                    dve.scalar_tensor_tensor(finished[q], bank[7][:, D:2 * D], 1.0 / SCALE, tile_of(xr, t), ALU.mult, ALU.add)
                    dve.drain()
                    dve.scalar_tensor_tensor(finished[q], bank[7][:, 0:D], invT[:, bass.ds(t, 1)], finished[q],
                                             ALU.mult, ALU.add).then_inc(s_res, 1)

                def tile(t, i, par, first=False, last=False):
                    for s in range(ST):
                        if not last:
                            one_hots(t + 1, s)
                        if s == 1 and not first:
                            sum_parts(t - 1, 1 - par)
                        if s == 5 and not first:
                            result(t - 1, i, 1 - par)

                for s in range(ST):
                    one_hots(0, s)
                tile(0, 0, 0, first=True)
                tile(1, 0, 1)
                tile(2, 0, 0)
                with dve.Fori(1, TN // 2 - 1) as i:
                    tile(2 * i + 1, i, 1)
                    tile(2 * i + 2, i, 0)
                tile(TN - 2, TN // 2 - 1, 1)
                tile(TN - 1, TN // 2 - 1, 0, last=True)
                sum_parts(TN - 1, 0)
                result(TN - 1, TN // 2, 0)
            with dve.Else():
                dve.wait_ge(n_table, 16)
                dve.memset(sumT, 0.0)
                dve.wait_ge(n_raw, 6 * 16)
                for k in range(2):
                    for b, m in ((0, G0), (1, G1)):
                        dve.tensor_copy(raw1[0:m, k, b, :], raw1i[0:m, k, b, :])
                dve.drain()
                dve.nop().then_inc(n_rawf, 1)

                def self_add(t):
                    dve.wait_ge(n_selfp, t + 1)
                    v = tile_of(xr, t)
                    dve.scalar_tensor_tensor(v, bank[5][:, 0:D], 1.0 / SCALE, v, ALU.mult, ALU.add).then_inc(n_self, 1)
                    dve.drain()
                    dve.tensor_tensor(v, v, bsbc[:, :], ALU.add)

                loop(dve, self_add, 0, TN)
                dve.wait_ge(s_masked, 3)
                with dve.Fori(0, G) as g:
                    dve.memset(wstart[:, :], 0.0)
                    dve.drain()
                    with dve.Fori(0, NW) as w:
                        dve.tensor_scalar(relw[:, :], tile_of(dstT1, g), wstart[:, 0:1], None, ALU.subtract)
                        dve.drain()
                        dve.tensor_scalar(wstart[:, :], wstart[:, :], float(WIN), None, ALU.add)
                        in_window(oneb, relw[:, :]).then_inc(n_oneb, 1)
                        dve.wait_ge(n_sum, g * NW + w + 1)
                        add_window(sumT, w * WIN, bank[0][:, 0:DH * WIN].rearrange("p (h w) -> p h w", h=DH))
                        dve.drain()
                    dve.nop().then_inc(n_group, 1)
                dve.drain()
                dve.nop().then_inc(n_done, 1)

                def any_result(t):
                    dve.wait_ge(n_neighp, t + 1)
                    if later(t):
                        dve.wait_ge(n_out, 16 * t)
                    dve.scalar_tensor_tensor(hbuf[:, 0, 0, :], bank[6][:, 0:D], invT[:, bass.ds(t, 1)], tile_of(xr, t),
                                             ALU.mult, ALU.add).then_inc(n_res, 1)

                any_result(0)
                loop(dve, any_result, 1, TN)


_INS = ["x", "src", "dst", "edge_attr_64", "L0_gnn_W1", "L0_gnn_b1", "L0_gnn_W2", "L0_gnn_b2",
        "L1_gnn_w_neigh", "L1_gnn_w_self", "L1_gnn_b_self"]
_TRANSPOSED = ("L1_gnn_w_neigh", "L1_gnn_w_self")


def kernel(**inputs):
    import numpy as _np
    import concourse.bacc as _bacc
    from concourse import mybir as _mybir
    from concourse.bass_utils import run_bass_kernel_spmd as _run

    nc = _bacc.Bacc("TRN2", target_bir_lowering=False, num_devices=1)
    arrays, args = {}, []
    for name in _INS:
        a = _np.asarray(inputs[name])
        a = _np.ascontiguousarray(a.T if name in _TRANSPOSED else a)
        arrays[f"in_{name}_dram"] = a
        args.append(nc.dram_tensor(f"in_{name}_dram", a.shape, _mybir.dt.from_np(a.dtype), kind="ExternalInput").ap())
    n, d = inputs["x"].shape
    out = nc.dram_tensor("out_dram", (n, d), _mybir.dt.float32, kind="ExternalOutput").ap()
    gnn_kernel(nc, *args, out)
    r = _run(nc, [arrays], core_ids=[0])
    return r.results[0]["out_dram"]
```

```python
from contextlib import ExitStack

import numpy as np

import concourse.bass as bass
from concourse import mybir
from concourse.alu_op_type import AluOpType as ALU

ACT = mybir.ActivationFunctionType
AX = mybir.AxisListType
F32 = mybir.dt.float32
F16 = mybir.dt.float16
BF16 = mybir.dt.bfloat16
I32 = mybir.dt.int32
U32 = mybir.dt.uint32

P = 128


def gnn_kernel(nc, x, src, dst, edges, w1, b1, w2, b2, wneighT, wselfT, bself, out):
    N, D = x.shape
    E, FE = edges.shape
    HID = w1.shape[1]
    DH = D // P
    HB = HID // P
    CH = 8
    GE = CH * P
    G = -(-E // GE)
    GF = G - 1
    REPEATED = GF * GE - (E - GE)
    G0 = min(G, P)
    G1 = G - G0
    T = 2 * (-(-N // (2 * P)))
    NP = T * P
    TF = N // P
    REST = N - TF * P
    TN = TF + 1
    U = T // 2
    WIN = 48
    NW = -(-N // WIN)
    SLOTS = 6
    PARTS = 3
    FULL = G // SLOTS
    TAIL = G - FULL * SLOTS
    LAG = PARTS - 1
    H0 = 7, 7 + U
    XL = 8
    XPARTS = TF // XL
    SPAN = 3
    BODIES = (FULL - H0[0]) // SPAN
    REMAIN = G - (H0[0] + BODIES * SPAN) * SLOTS
    BESIDE = BODIES
    NEED = -(-4 * P // (SPAN * SLOTS))
    LIMIT = NEED, 4 * P - NEED * SLOTS * H0[0]
    NM = 2 * P
    SL = P
    CB = NP // 2 // P
    CT = P // 2
    KEYS = 2 * TN
    SC = 8
    ST = CT // SC
    BC = SC // 2
    KB = 5
    KEY0 = U // 2 - 3
    NOKEY = 1024.0
    SCALE = 2048.0
    EPS = 1e-5
    assert 0 < TAIL < SLOTS and G1 < P and FULL > H0[1] and U % SPAN == 1 and U % 2 == 1
    assert TF % XL == 0 and XPARTS < H0[0] and FE == 64 and NP >= N + WIN and 2 * P >= NEED * LAG
    assert TN % 4 == 1 and T == TN + 1 and CB % KB == 0 and CB == U and BC * KEYS <= 512
    assert KEY0 == BESIDE + 1 and CB // KB == 5 and E < 2 ** 24

    ctx = ExitStack()
    with ctx:
        def sb(name, shape, dt):
            return ctx.enter_context(nc.sbuf_tensor(name, shape, dt))

        def sem(name):
            return ctx.enter_context(nc.semaphore(name))

        def sems(name, n=2):
            return [sem(f"{name}{q}") for q in range(n)]

        table = nc.dram_tensor("h1_table", (NP, 2 * D), F16).ap()

        xr = sb("xr", [P, T, D], F32)
        hreg = sb("hreg", [P, T, D], F32)
        h0T = hreg[:, :, :].rearrange("p t (h n) -> p t h n", h=DH)
        htab = hreg[:, :, :].rearrange("p t d -> p (t d)").bitcast(F16).rearrange("p (t d) -> p t d", t=T)
        sumT = hreg[:, :, :].rearrange("p t d -> p (t d)").rearrange("p (h n) -> p h n", h=DH)
        areg = sb("areg", [P, NP], F32)
        acc = areg
        adj = areg[:, :].bitcast(BF16)[:, 0:2 * P * TN].rearrange("p (q n h) -> p q n h", q=2, n=P)
        rs1 = sb("rs1", [P, T], F32)
        nm1 = sb("nm1", [P, T], F32)
        cntN = sb("cntN", [P, T], F32)
        invT = sb("invT", [P, T], F32)
        relT = sb("relT", [P, G, CH], F32)
        base = sb("base", [1, G], I32)
        flag = sb("flag", [1, 2], I32)
        kreg = sb("kreg", [P, 2, CB, SL], I32)
        pairs16 = kreg[:, :, :, :].rearrange("p k b s -> p (k b s)").bitcast(F16).rearrange(
            "p (k j d) -> p k j d", k=2, d=2)
        w1a = sb("w1a", [FE, HID], F32)
        w1b = sb("w1b", [P, DH, HID], F32)
        w2s = sb("w2s", [P, HB, D], F32)
        wns = sb("wns", [P, DH, D], F32)
        wss = sb("wss", [P, DH, D], F32)
        b1T = sb("b1T", [P, HB], F32)
        b2bc = sb("b2bc", [P, D], F32)
        bsbc = sb("bsbc", [P, D], F32)
        ident = sb("ident", [P, P], F32)
        ident16 = sb("ident16", [P, P], F16)
        ones = sb("ones", [P, P], F32)
        iota = sb("iota", [P, WIN], F32)
        iota16 = sb("iota16", [P, P], F16)
        below = sb("below", [P, 2, P], F32)
        tiles_before = sb("tiles_before", [T, CB], F32)
        node0 = sb("node0", [P, CB], F32)
        oreg = sb("oreg", [P, 2, KB * SL], F32)
        more = sb("more", [P, 2, KB * SL], F16)
        hbuf = sb("hbuf", [P, 2, 2, D], F32)
        hids = sb("hids", [P, 2, HB, NM], F32)
        deg = sb("deg", [FE, NM], F32)
        h0buf = sb("h0buf", [P, 2, D], F32)
        aggn = sb("aggn", [FE, 2, NM], F32)
        st6 = sb("st6", [P, 2, 2, 6], F32)
        mv = sb("mv", [P, 2, 2, 2], F32)
        ve = sb("ve", [P, 2, 2], F32)
        sd = sb("sd", [P, 2, 2], F32)
        rsq = sb("rsq", [P, 2, 2], F32)
        nmq = sb("nmq", [P, 2, 2], F32)
        epst = sb("epst", [P, 1], F32)
        ln0 = sb("ln0", [P, 6, T], F32)
        viol = sb("viol", [P, 11], F32)
        limit = sb("limit", [P, 2], F32)
        noplace = sb("noplace", [P, CB // KB], F32)
        wstart = sb("wstart", [P, 1], F32)
        relw = sb("relw", [P, CH], F32)
        tot = sb("tot", [T, 1], F32)
        totb = sb("totb", [T, CB], F32)
        startu = sb("startu", [P, CB], U32)
        key, away = oreg[:, 0, :], oreg[:, 1, :]
        wspace = relT[:, :, :].rearrange("p g c -> p (g c)")
        khi = wspace[:, 0:KB * SL].bitcast(I32)
        key16 = [wspace[:, KB * SL:2 * KB * SL].bitcast(F16)[:, 0:KB * SL], more[:, 0, :]]
        lo16 = [wspace[:, KB * SL:2 * KB * SL].bitcast(F16)[:, KB * SL:2 * KB * SL], more[:, 1, :]]
        h16 = hids[:, :, :, :].rearrange("p a b n -> p (a b n)").bitcast(BF16)
        onesrc = h16[:, 0:2 * SC * P].rearrange("p (q c n) -> p q c n", q=2, c=SC)
        onekey = h16[:, 2 * SC * P:2 * SC * (P + KEYS)].rearrange("p (q c k) -> p q c k", q=2, c=SC)
        layer1 = oreg[:, :, :].rearrange("p a b -> p (a b)")
        sumN = layer1[:, 0:D]
        h1buf = layer1[:, D:2 * D]
        bothT = hbuf[:, 1, :, :].rearrange("p k d -> p (k d)")
        finished = [hbuf[:, 0, q, :] for q in range(2)]
        space = kreg[:, :, :, :].rearrange("p k b s -> p (k b s)")
        slot = CH * FE
        words = [space[:, a * slot:b * slot] for a, b in
                 ((0, SLOTS), (SLOTS, SLOTS + PARTS), (SLOTS + PARTS, SLOTS + 2 * PARTS))]
        edg, rest = (v.bitcast(F32).rearrange("p (q c f) -> p q c f", c=CH, f=FE) for v in words[0:2])
        low = words[2].bitcast(BF16).rearrange("p (q c f) -> p q c f", q=PARTS, c=CH)
        edg_top, rest_top = (v.bitcast(BF16).rearrange("p (q c f d) -> p q c f d", c=CH, f=FE, d=2)[:, :, :, :, 1]
                             for v in words[0:2])
        oneh = oreg[:, :, :].rearrange("p a b -> p (a b)").bitcast(BF16)[:, 0:PARTS * CH * WIN].rearrange(
            "p (q c w) -> p q c w", q=PARTS, c=CH)
        relP = relT[:, :, :].rearrange("p g c -> p (g c)").bitcast(F16).rearrange("p (g c d) -> p g c d", g=G, d=2)
        rawi = hreg[:, :, :].rearrange("p t d -> p (t d)").bitcast(I32)[:, 0:2 * GE].rearrange("p (b j) -> p b j", b=2)
        raw = hreg[:, :, :].rearrange("p t d -> p (t d)")[:, 0:2 * GE].rearrange("p (b j) -> p b j", b=2)
        relr = hids[:, :, :, :].rearrange("p a b n -> p (a b n)").rearrange("p (b j) -> p b j", b=2)
        dstT0 = hids[:, :, :, :].rearrange("p a b n -> p (a b n)")[:, 0:G * CH].rearrange("p (g c) -> p g c", c=CH)
        rows = kreg[:, :, :, :].rearrange("p k b s -> p (k b s)").bitcast(F16)[:, 0:CH * 2 * D].rearrange(
            "p (c d) -> p c d", c=CH)
        srcT = kreg[:, :, :, :].rearrange("p k b s -> p (k b s)")[:, 4 * GE:4 * GE + G * CH].bitcast(U32).rearrange(
            "p (g c) -> p g c", c=CH)
        raw1 = areg[:, 0:4 * GE].rearrange("p (k b j) -> p k b j", k=2, b=2)
        raw1i = areg[:, 0:4 * GE].bitcast(I32).rearrange("p (k b j) -> p k b j", k=2, b=2)
        dstT1 = areg[:, 4 * GE:4 * GE + G * CH].rearrange("p (g c) -> p g c", c=CH)
        oneb = oneh[:, 0, :, :]
        stage = sb("stage", [P, CH], U32)

        cpl = [ctx.enter_context(nc.psum_tensor(f"couples{n}", [P, 2, 512], F32)) for n in range(2)]
        bank = [cpl[0][:, 0, :], cpl[0][:, 1, :], cpl[1][:, 0, :], cpl[1][:, 1, :]]
        bank16 = bank[1].bitcast(F16)
        bank += [ctx.enter_context(nc.psum_tensor(f"bank{n}", [P, 512], F32))[:, :] for n in range(4, 8)]

        s_raw = sem("s_raw")
        s_x = sems("s_x_", XPARTS)
        s_w = sem("s_w")
        s_zero = sem("s_zero")
        s_const = sem("s_const")
        s_viol = sem("s_viol")
        s_violT = sem("s_violT")
        s_flag = sem("s_flag")
        s_rel = sem("s_rel")
        s_idx_tr = sem("s_idx_tr")
        s_idx_act = sem("s_idx_act")
        s_masked = sem("s_masked")
        s_sd0 = sem("s_sd0")
        s_ln0 = sem("s_ln0")
        s_h0 = sem("s_h0")
        s_h0tr = sem("s_h0tr")
        s_h0T = sem("s_h0T")
        s_b2 = sem("s_b2")
        s_edges = sems("s_edges_", SLOTS)
        s_oneh = sems("s_oneh_", SLOTS)
        s_rest = sems("s_rest_", SLOTS)
        s_low = sems("s_low_", SLOTS)
        s_esum = sems("s_esum_", SLOTS)
        s_added = sems("s_added_", SLOTS)
        s_acc = sem("s_acc")
        s_cntp = sem("s_cntp")
        s_cnt = sem("s_cnt")
        s_cntT = sem("s_cntT")
        s_totb = sem("s_totb")
        s_startp = sem("s_startp")
        s_start = sem("s_start")
        s_places = sem("s_places")
        s_keys = sem("s_keys")
        s_keytr = sem("s_keytr")
        s_lotr = sem("s_lotr")
        s_keyT = sem("s_keyT")
        s_loT = sem("s_loT")
        s_nopl = sem("s_nopl")
        s_noplp = sem("s_noplp")
        s_flag1 = sem("s_flag1")
        s_agg = sems("s_agg_")
        s_hidp = sems("s_hidp_")
        s_hids = sems("s_hids_")
        s_outp = sems("s_outp_")
        s_x1 = sems("s_x1_")
        s_var1 = sems("s_var1_")
        s_sd1 = sems("s_sd1_")
        s_ln1 = sems("s_ln1_")
        s_hi = sems("s_hi_")
        s_tab = sems("s_tab_")
        s_one = sem("s_one")
        s_cplp = sem("s_cplp")
        s_adj = sem("s_adj")
        s_dense = sem("s_dense")
        s_sumN = sem("s_sumN")
        s_h1 = sem("s_h1")
        s_bs = sem("s_bs")
        s_trp = sem("s_trp")
        s_trs = sem("s_trs")
        s_outq = sem("s_outq")
        s_res = sem("s_res")
        s_out = sems("s_out_")
        a_tr = sem("a_tr")
        a_trc = sem("a_trc")
        a_edges = sem("a_edges")
        a_rest = sem("a_rest")
        a_low = sem("a_low")
        a_oneh = sem("a_oneh")
        a_sum = sem("a_sum")
        a_group = sem("a_group")
        n_raw = sem("n_raw")
        n_rawf = sem("n_rawf")
        n_tr = sem("n_tr")
        n_trc = sem("n_trc")
        n_table = sem("n_table")
        n_h = sem("n_h")
        n_hT = sem("n_hT")
        n_hTs = sem("n_hTs")
        n_selfp = sem("n_selfp")
        n_self = sem("n_self")
        n_stage = sem("n_stage")
        n_rows = sem("n_rows")
        n_oneb = sem("n_oneb")
        n_sum = sem("n_sum")
        n_group = sem("n_group")
        n_done = sem("n_done")
        n_sumc = sem("n_sumc")
        n_neighp = sem("n_neighp")
        n_res = sem("n_res")
        n_out = sem("n_out")

        def edge_rows(g):
            return edges[bass.ds(g * GE, GE), :].rearrange("(p c) f -> p (c f)", c=CH)

        last_edge_rows = edges[E - GE:E, :].rearrange("(p c) f -> p (c f)", c=CH)

        def in_windows(eng):
            eng.wait_ge(s_flag, 1)
            return eng.value_load(flag[0:1, 0:1], min_val=0, max_val=1) < 1

        def in_places(eng):
            eng.wait_ge(s_flag1, 1)
            return eng.value_load(flag[0:1, 1:2], min_val=0, max_val=1) < 1

        def later(i):
            return not isinstance(i, int) or i > 0

        def group_at(k, j):
            return H0[0] + SPAN * k + j // SLOTS, j % SLOTS

        def loop(eng, body, first, end, step=1):
            with eng.Fori(first, end, step) as i:
                body(i)

        def load_index_table(sp, into, done, v):
            sp.dma_start(into[0:G0, 0, :], v[0:G0 * GE].rearrange("(g j) -> g j", g=G0)).then_inc(done, 16)
            sp.dma_start(into[0:G1 - 1, 1, :], v[G0 * GE:GF * GE].rearrange("(g j) -> g j", g=G1 - 1)).then_inc(done, 16)
            sp.dma_start(into[G1 - 1:G1, 1, :], v[E - GE:E].rearrange("(g j) -> g j", g=1)).then_inc(done, 16)

        def transpose_table(pe, into, tab, c):
            for b, m in ((0, G0), (1, G1)):
                ins = pe.transpose(into[:, b * P:b * P + m],
                                   tab[0:m, b, :].rearrange("g (p c) -> g c p", c=CH)[:, c, :], ident[0:m, 0:m])
            return ins

        def mask_repeated(pool, v):
            return pool.affine_select(out=v, in_=v, compare_op=ALU.is_ge, fill=-NOKEY * 8, base=-REPEATED,
                                      pattern=[[1, CH]] + [[0, 2]] * (len(v.shape) - 2), channel_multiplier=CH)

        def tile_pairs(v, g):
            return v[:, bass.ds(g, 1), :, :].rearrange("p a c d -> p (a c) d")

        def tile_of(v, t):
            return v[:, bass.ds(t, 1), :].rearrange("p a d -> p (a d)")

        block = ctx.enter_context(nc.Block())

        @block.sync
        def _(sp):
            load_index_table(sp, rawi, s_raw, dst)
            with nc.allow_non_contiguous_dma(reason="one index of each group"):
                sp.dma_start(base[0:1, 0:GF], dst[0:GF * GE].rearrange("(g j) -> j g", g=GF)[0:1, :]).then_inc(s_raw, 16)
            sp.dma_start(base[0:1, GF:G], dst[E - GE:E - GE + 1].rearrange("(a b) -> a b", a=1)).then_inc(s_raw, 16)

            def load(i, q, rows_of=None):
                if later(i):
                    sp.wait_ge(s_esum[q], i)
                sp.dma_start(edg[:, q, :, :].rearrange("p c f -> p (c f)"),
                             edge_rows(SLOTS * i + q) if rows_of is None else rows_of).then_inc(s_edges[q], 16)

            for q in range(SLOTS):
                load(0, q)
            def load_x(part):
                t = part * XL
                sp.dma_start(xr[:, t:t + XL, :],
                             x[t * P:(t + XL) * P, :].rearrange("(t p) d -> p t d", p=P)).then_inc(s_x[part], 16)
                if part == XPARTS - 1:
                    sp.dma_start(xr[0:REST, TF, :], x[TF * P:N, :]).then_inc(s_x[part], 16)

            def load_weights():
                sp.dma_start(b2bc[:, :], b2.rearrange("(a n) -> a n", a=1).broadcast_to([P, D])).then_inc(s_w, 16)
                sp.dma_start(bsbc[:, :], bself.rearrange("(a n) -> a n", a=1).broadcast_to([P, D])).then_inc(s_w, 16)
                sp.dma_start(w1a[:, :], w1[0:FE, :]).then_inc(s_w, 16)
                sp.dma_start(w1b[:, :, :], w1[FE:FE + D, :].rearrange("(h p) n -> p h n", p=P)).then_inc(s_w, 16)
                sp.dma_start(w2s[:, :, :], w2.rearrange("(h p) n -> p h n", p=P)).then_inc(s_w, 16)
                sp.dma_start(wns[:, :, :], wneighT.rearrange("(h p) n -> p h n", p=P)).then_inc(s_w, 16)
                sp.dma_start(wss[:, :, :], wselfT.rearrange("(h p) n -> p h n", p=P)).then_inc(s_w, 16)
                with nc.allow_non_contiguous_dma(reason="a bias on the partitions"):
                    sp.dma_start(b1T[:, :], b1.rearrange("(h p) -> p h", p=P)).then_inc(s_w, 16)

            sp.wait_ge(s_zero, 1)
            load_x(0)
            with sp.If(in_windows(sp)):
                def load_slots(i):
                    for q in range(SLOTS):
                        load(i, q)

                for i in range(1, H0[0]):
                    load_slots(i)
                    if i < XPARTS:
                        load_x(i)
                load_weights()
                loop(sp, load_slots, H0[0], FULL)
                for q in range(TAIL - 1):
                    load(FULL, q)
                load(FULL, TAIL - 1, last_edge_rows)
            with sp.Else():
                for part in range(1, XPARTS):
                    load_x(part)
                load_weights()

                def load_any(g, rows_of=None):
                    sp.wait_ge(a_group, g)
                    sp.dma_start(edg[:, 0, :, :].rearrange("p c f -> p (c f)"),
                                 edge_rows(g) if rows_of is None else rows_of).then_inc(a_edges, 16)

                loop(sp, load_any, 1, GF)
                load_any(GF, last_edge_rows)

            with sp.If(in_places(sp)):
                def result(i, q, n=P):
                    sp.wait_ge(s_res, 2 * i + q + 1)
                    sp.dma_start(out[bass.ds((2 * i + q) * P, n), :], finished[q][0:n, :]).then_inc(s_out[q], 16)

                def two(i):
                    result(i, 0)
                    result(i, 1)

                loop(sp, two, 0, TF // 2)
                result(TF // 2, 0, REST)
                sp.wait_ge(s_out[0], 16 * (TF // 2 + 1))
                sp.wait_ge(s_out[1], 16 * (TF // 2))
            with sp.Else():
                sp.wait_ge(s_adj, ST)
                sp.wait_ge(s_tab[0], U // 2 + 1)
                sp.wait_ge(s_tab[1], U // 2)
                sp.dma_start(table.rearrange("(t p) d -> p t d", p=P), htab).then_inc(n_table, 16)
                load_index_table(sp, raw1i[:, 0], n_raw, dst)
                load_index_table(sp, raw1i[:, 1], n_raw, src)

                def any_result(t, n=P):
                    sp.wait_ge(n_res, t + 1)
                    sp.dma_start(out[bass.ds(t * P, n), :], hbuf[0:n, 0, 0, :]).then_inc(n_out, 16)

                loop(sp, any_result, 0, TF)
                any_result(TF, REST)
                sp.wait_ge(n_out, 16 * TN)

        @block.gpsimd
        def _(pool):
            pool.memset(xr[:, TF:T, :], 0.0).then_inc(s_zero, 1)
            pool.memset(viol[:, :], 0.0)
            pool.memset(epst[:, :], EPS)
            pool.memset(ident[:, :], 0.0)
            pool.memset(ones[:, :], 1.0)
            pool.memset(below[:, :, :], 0.0)
            pool.memset(tiles_before[:, :], 0.0)
            pool.iota(iota[:, :], pattern=[[1, WIN]], base=0, channel_multiplier=0,
                      allow_small_or_imprecise_dtypes=True)
            pool.iota(iota16[:, :], pattern=[[1, P]], base=0, channel_multiplier=0,
                      allow_small_or_imprecise_dtypes=True)
            pool.iota(limit[:, :], pattern=[[LIMIT[0] * P, 2]], base=LIMIT[1], channel_multiplier=LIMIT[0],
                      allow_small_or_imprecise_dtypes=True)
            pool.iota(node0[:, :], pattern=[[2 * P, CB]], base=0, channel_multiplier=2,
                      allow_small_or_imprecise_dtypes=True)
            pool.drain()
            pool.affine_select(out=ident[:, :], in_=ident[:, :], compare_op=ALU.not_equal, fill=1.0,
                               base=0, pattern=[[-1, P]], channel_multiplier=1)
            pool.drain()
            pool.tensor_copy(ident16[:, :], ident[:, :])
            for k in range(2):
                pool.affine_select(out=below[:, k, :], in_=below[:, k, :], compare_op=ALU.is_ge, fill=1.0,
                                   base=k * P, pattern=[[-2, P]], channel_multiplier=1)
            pool.affine_select(out=tiles_before[:, :], in_=tiles_before[:, :], compare_op=ALU.is_ge, fill=1.0,
                               base=0, pattern=[[-2, CB]], channel_multiplier=1).then_inc(s_const, 1)
            pool.memset(low[:, :, :, :].rearrange("p q c f -> p (q c f)"), 1.0)
            pool.memset(acc[:, :], 0.0).then_inc(s_const, 1)
            pool.wait_ge(s_idx_act, CH)
            mask_repeated(pool, relP[:, GF, :, :]).then_inc(s_masked, 1)

            def add_b2(u):
                pool.wait_ge(s_h0, 2 * u + 2)
                v = xr[:, bass.ds(2 * u, 2), :]
                pool.tensor_tensor(v, v, b2bc[:, :].unsqueeze(1).broadcast_to([P, 2, D]), ALU.add).then_inc(s_b2, 1)

            def low_of(q):
                return pool.tensor_tensor(low[:, q, :, 0:FE], rest[:, q, :, :], rest_top[:, q, :, :], ALU.subtract)

            with pool.If(in_windows(pool)):
                def low_part(i, q):
                    pool.wait_ge(s_rest[q], i + 1)
                    low_of(q % PARTS).then_inc(s_low[q], 1)

                def low_parts(i):
                    for q in range(SLOTS):
                        low_part(i, q)

                def with_b2(i):
                    low_parts(i)
                    add_b2(i - H0[0])

                loop(pool, low_parts, 0, H0[0])
                pool.wait_ge(s_w, 8 * 16)
                loop(pool, with_b2, H0[0], H0[1])
                loop(pool, low_parts, H0[1], FULL)
                for q in range(TAIL):
                    low_part(FULL, q)
            with pool.Else():
                pool.wait_ge(a_trc, CH)
                mask_repeated(pool, dstT0[:, GF, :]).then_inc(s_masked, 1)
                pool.wait_ge(s_w, 8 * 16)
                loop(pool, add_b2, 0, U)

                def any_low(g):
                    pool.wait_ge(a_rest, g + 1)
                    low_of(0).then_inc(a_low, 1)

                loop(pool, any_low, 0, G)

            pool.wait_ge(s_start, 1)
            for b in range(CB):
                for k, v in enumerate((dst, src)):
                    pool.indirect_dma_start(kreg[:, k, b, :], None, v.rearrange("(e a) -> e a", a=1),
                                            bass.IndirectOffsetOnAxis(ap=startu[:, b:b + 1], axis=0)).then_inc(s_places, 16)
                if b % KB == KB - 1:
                    pool.wait_ge(s_places, 16 * 2 * (b + 1))

            with pool.If(in_places(pool)):
                def add_bs(t):
                    pool.wait_ge(s_h1, t + 1)
                    v = tile_of(xr, t)
                    pool.tensor_tensor(v, v, bsbc[:, :], ALU.add).then_inc(s_bs, 1)

                loop(pool, add_bs, 0, TN)
            with pool.Else():
                pool.wait_ge(n_trc, 2 * CH)
                mask_repeated(pool, dstT1[:, GF, :]).then_inc(s_masked, 2)

                def any_group(n):
                    pool.wait_ge(n_table, 16)
                    pool.wait_ge(n_stage, n)
                    for c in range(CH):
                        pool.indirect_dma_start(rows[:, c, :], None, table,
                                                bass.IndirectOffsetOnAxis(ap=stage[:, c:c + 1], axis=0)).then_inc(n_rows, 16)

                loop(pool, any_group, 1, G + 1)

        @block.scalar
        def _(act):
            for c in range(CH):
                act.wait_ge(s_idx_tr, c + 1)
                act.activation(relP[:, :, c, :], bank[c % 2][:, 0:G].unsqueeze(2).broadcast_to([P, G, 2]),
                               ACT.Copy).then_inc(s_idx_act, 1)

            unused = hids[:, :, :, :].rearrange("p q b n -> p (q b) n")

            def passes(part):
                lo, hi = part * XL, (part + 1) * XL if part < XPARTS - 1 else T
                act.wait_ge(s_x[part], 32 if part == XPARTS - 1 else 16)
                for t in range(lo, hi):
                    if t % 8 == 0:
                        act.drain()
                    act.activation(unused[:, t % 8, :], xr[:, t, :], ACT.Copy, accum_out=ln0[:, 0, t:t + 1])
                act.drain()
                act.activation(ln0[:, 1, lo:hi], ln0[:, 0, lo:hi], ACT.Copy, scale=-1.0 / D)
                act.drain()
                for t in range(lo, hi):
                    if t % 8 == 0 and t > lo:
                        act.drain()
                    act.activation(unused[:, t % 8, :], xr[:, t, :], ACT.Square, bias=ln0[:, 1, t:t + 1], scale=1.0,
                                   accum_out=ln0[:, 2, t:t + 1])

            act.wait_ge(s_viol, 1)
            for part in range(XPARTS):
                passes(part)
            act.drain()
            act.activation(ln0[:, 3, :], ln0[:, 2, :], ACT.Sqrt, bias=epst[:, 0:1], scale=1.0 / D).then_inc(s_sd0, 1)

            def hidden(i, q, own=0):
                if later(i):
                    act.wait_ge(s_outp[q], i)
                for k in range(2):
                    act.wait_ge(s_hidp[q], 2 * i + k + 1)
                    for b in range(2):
                        ins = act.activation(hids[:, q, 2 * k + b, :], bank[4 + k - 2 * q * own][:, b * NM:(b + 1) * NM],
                                             ACT.Relu, bias=b1T[:, 2 * k + b:2 * k + b + 1])
                    ins.then_inc(s_hids[q], 1)

            def sd_of(i, q):
                act.wait_ge(s_var1[q], i + 1)
                act.activation(sd[:, q, :], ve[:, q, :], ACT.Sqrt).then_inc(s_sd1[q], 1)

            def h1(i, q):
                u = 2 * i + q
                act.wait_ge(s_ln1[q], i + 1)
                act.activation(rs1[:, bass.ds(2 * u, 2)], rsq[:, q, :], ACT.Copy)
                act.activation(nm1[:, bass.ds(2 * u, 2)], nmq[:, q, :], ACT.Copy)
                if later(i):
                    act.wait_ge(s_tab[q], i)
                for t in range(2):
                    act.activation(hbuf[:, q, t, :], tile_of(xr, 2 * u + t),
                                   ACT.Relu, bias=nmq[:, q, t:t + 1], scale=rsq[:, q, t:t + 1])
                act.drain()
                act.activation(htab[:, bass.ds(2 * u, 2), 0:D], hbuf[:, q, :, :], ACT.Copy).then_inc(s_hi[q], 1)

            def h0(u):
                if later(u):
                    act.wait_ge(s_h0tr, u)
                else:
                    act.wait_ge(s_ln0, 1)
                for t in range(2):
                    act.activation(h0buf[:, t, :], tile_of(xr, 2 * u + t), ACT.Relu, bias=ln0[:, 5, bass.ds(2 * u + t, 1)],
                                   scale=ln0[:, 4, bass.ds(2 * u + t, 1)]).then_inc(s_h0, 1)

            def copy_h0(u):
                act.wait_ge(s_h0tr, u + 1)
                act.activation(h0T[:, bass.ds(2 * u, 2), :, :],
                               bank[3].rearrange("p (t h n) -> p t h n", t=2, h=DH), ACT.Copy).then_inc(s_h0T, 1)

            with act.If(in_windows(act)):
                def span(k, pairs=SPAN):
                    begun, due = (not isinstance(k, int) or k >= back for back in (1, 2))
                    if due:
                        h1(k - 2, 0)
                    h0(SPAN * k)
                    if begun:
                        hidden(k - 1, 0)
                    if due:
                        sd_of(k - 2, 1)
                    copy_h0(SPAN * k)
                    if due:
                        h1(k - 2, 1)
                    if pairs > 1:
                        h0(SPAN * k + 1)
                    if begun:
                        hidden(k - 1, 1)
                    if pairs > 1:
                        copy_h0(SPAN * k + 1)
                        h0(SPAN * k + 2)
                    if begun:
                        sd_of(k - 1, 0)
                    if pairs > 1:
                        copy_h0(SPAN * k + 2)

                for k in range(3):
                    span(k)
                loop(act, span, 3, BODIES)
                span(BODIES, pairs=1)
                h1(BODIES - 1, 0)
                sd_of(BODIES - 1, 1)
                h1(BODIES - 1, 1)
            with act.Else():
                for c in range(CH):
                    act.wait_ge(a_tr, c + 1)
                    act.activation(dstT0[:, :, c], bank[c % 2][:, 0:G], ACT.Copy).then_inc(a_trc, 1)

                def both_h0(u):
                    h0(u)
                    copy_h0(u)

                both_h0(0)
                loop(act, both_h0, 1, U)
                def any_layer0(i):
                    hidden(i, 0)
                    hidden(i, 1)
                    for q in range(2):
                        sd_of(i, q)
                    for q in range(2):
                        h1(i, q)

                any_layer0(0)
                loop(act, any_layer0, 1, BESIDE)

            def copy_keys(n):
                act.wait_ge(s_keytr, n + 1)
                act.activation(pairs16[:, 0, bass.ds(n * KB * P, KB * P), :],
                               bank16[:, 0:KB * P].unsqueeze(2).broadcast_to([P, KB * P, 2]), ACT.Copy).then_inc(s_keyT, 1)

            def copy_places(n):
                act.wait_ge(s_lotr, n + 1)
                act.activation(pairs16[:, 1, bass.ds(n * KB * P, KB * P), :],
                               bank16[:, 0:KB * P].unsqueeze(2).broadcast_to([P, KB * P, 2]), ACT.Copy).then_inc(s_loT, 1)

            def layer0(i, n=None):
                hidden(i, 0)
                hidden(i, 1, own=1)
                if n is not None:
                    copy_keys(n)
                for q in range(2):
                    sd_of(i, q)
                for q in range(2):
                    h1(i, q)
                if n is not None:
                    copy_places(n)

            loop(act, layer0, BESIDE, KEY0)
            for n in range(3):
                layer0(KEY0 + n, n)
            hidden(U // 2, 0)
            copy_keys(3)
            copy_places(3)
            sd_of(U // 2, 0)
            h1(U // 2, 0)
            copy_keys(4)
            copy_places(4)
            act.wait_ge(s_tab[0], U // 2 + 1)
            act.wait_ge(s_tab[1], U // 2)

            def copy_counts(t, par, s):
                act.wait_ge(s_cplp, t * ST + s + 1)
                step = adj[:, par, :, :].rearrange("p n h -> p (n h)")[:, s * SC * KEYS:(s + 1) * SC * KEYS]
                act.activation(step.rearrange("p (a k) -> p a k", a=2),
                               cpl[s % 2][:, :, 0:BC * KEYS], ACT.Copy).then_inc(s_adj, 1)

            def h1_tile(t):
                if later(t):
                    act.wait_ge(s_trp, t)
                act.activation(h1buf[:, :], tile_of(xr, t), ACT.Relu,
                               bias=nm1[:, bass.ds(t, 1)], scale=rs1[:, bass.ds(t, 1)]).then_inc(s_h1, 1)

            def copy_transposed(t):
                act.wait_ge(s_trp, t + 1)
                if later(t):
                    act.wait_ge(s_outq, t)
                act.activation(bothT, bank[6][:, :], ACT.Copy).then_inc(s_trs, 1)

            for s in range(ST):
                copy_counts(0, 0, s)
            with act.If(in_places(act)):
                def tile(t, par, first=False, last=False):
                    if not first and not last:
                        act.wait_ge(s_dense, t)
                    for s in range(ST):
                        if not last:
                            copy_counts(t + 1, 1 - par, s)
                        if s == 1 and not first:
                            h1_tile(t - 1)
                        if s == 3 and not first:
                            copy_transposed(t - 1)

                tile(0, 0, first=True)
                tile(1, 1)
                tile(2, 0)
                with act.Fori(0, TN // 4 - 1) as i:
                    for t in range(3, 7):
                        tile(4 * i + t, t % 2)
                tile(TN - 2, 1)
                tile(TN - 1, 0, last=True)
                h1_tile(TN - 1)
                copy_transposed(TN - 1)
            with act.Else():
                for c in range(CH):
                    for k in range(2):
                        act.wait_ge(n_tr, 2 * c + k + 1)
                        act.activation((dstT1, srcT)[k][:, :, c], bank[2 * k + c % 2][:, 0:G], ACT.Copy).then_inc(n_trc, 1)

                def self_part(t):
                    if later(t):
                        act.wait_ge(n_hT, t)
                    act.activation(hbuf[:, 0, 0, :], tile_of(xr, t), ACT.Relu,
                                   bias=nm1[:, bass.ds(t, 1)], scale=rs1[:, bass.ds(t, 1)]).then_inc(n_h, 1)
                    act.wait_ge(n_hT, t + 1)
                    if later(t):
                        act.wait_ge(n_selfp, t)
                    act.activation(hbuf[:, 0, 1, :], bank[4][:, 0:D], ACT.Copy).then_inc(n_hTs, 1)

                self_part(0)
                loop(act, self_part, 1, TN)

                def any_src(g):
                    if later(g):
                        act.wait_ge(n_group, g)
                    act.activation(stage[:, :], tile_of(srcT, g), ACT.Copy).then_inc(n_stage, 1)

                any_src(0)
                loop(act, any_src, 1, G)

                act.wait_ge(n_done, 1)

                def copy_sums(t):
                    if later(t):
                        act.wait_ge(n_neighp, t)
                    act.activation(hids[:, 0, 0, :].rearrange("p (h n) -> p h n", h=DH),
                                   sumT[:, :, bass.ds(t * P, P)], ACT.Copy).then_inc(n_sumc, 1)

                copy_sums(0)
                loop(act, copy_sums, 1, TN)

        @block.tensor
        def _(pe):
            pe.wait_ge(s_const, 1)
            pe.wait_ge(s_rel, 1)
            for c in range(CH):
                if c >= 2:
                    pe.wait_ge(s_idx_act, c - 1)
                transpose_table(pe, bank[c % 2], relr, c).then_inc(s_idx_tr, 1)
            pe.wait_ge(s_viol, 1)
            pe.transpose(bank[7][0:1, 0:P], viol[:, 0:1], ident[:, :]).then_inc(s_violT, 1)

            def h0tr(u):
                pe.wait_ge(s_h0, 2 * u + 2)
                if later(u):
                    pe.wait_ge(s_h0T, u)
                for t in range(2):
                    for h in range(DH):
                        ins = pe.transpose(bank[3][:, (t * DH + h) * P:(t * DH + h + 1) * P],
                                           h0buf[:, t, h * P:(h + 1) * P], ident[:, :])
                ins.then_inc(s_h0tr, 1)

            def edge_sums(into, q):
                k = q % PARTS
                pe.matmul(into[:, 0:WIN], low[:, k, 0, :], oneh[:, k, 0, :], start=True, stop=False)
                for part in (edg_top[:, q], rest_top[:, k]):
                    for c in range(CH):
                        pe.matmul(into[0:FE, 0:WIN], part[:, c, :], oneh[:, k, c, :], start=False, stop=False)
                for c in range(1, CH):
                    ins = pe.matmul(into[:, 0:WIN], low[:, k, c, :], oneh[:, k, c, :], start=False, stop=(c == CH - 1))
                return ins

            def hidden(i, q, k, own=0):
                u = 2 * i + q
                if k == 0:
                    pe.wait_ge(s_agg[q], i + 1)
                    pe.wait_ge(s_h0T, 2 * i + q + 1)
                if own:
                    pe.wait_ge(s_hids[q], 2 * i + (k - 1))
                elif q == 1:
                    pe.wait_ge(s_hids[0], 2 * i + (k + 1))
                elif later(i):
                    pe.wait_ge(s_hids[1], 2 * i + (k - 1))
                for b in range(2):
                    o = bank[4 + k - 2 * q * own][:, b * NM:(b + 1) * NM]
                    cols = slice((2 * k + b) * P, (2 * k + b + 1) * P)
                    pe.matmul(o, w1a[:, cols], aggn[:, q, :], start=True, stop=False)
                    for h in range(DH):
                        ins = pe.matmul(o, w1b[:, h, cols], h0T[:, bass.ds(2 * u, 2), h, :], start=False, stop=(h == DH - 1))
                ins.then_inc(s_hidp[q], 1)

            def outer(i, q, t):
                if t == 0:
                    if later(i):
                        pe.wait_ge(s_x1[q], i)
                    pe.wait_ge(s_hids[q], 2 * i + 2)
                for b in range(HB):
                    ins = pe.matmul(bank[6 + q][:, t * D:(t + 1) * D], hids[:, q, b, t * P:(t + 1) * P], w2s[:, b, :],
                                    start=(b == 0), stop=(b == HB - 1))
                if t == 1:
                    ins.then_inc(s_outp[q], 1)

            parts = {0: (hidden, 0, 0), 2: (hidden, 0, 1), 4: (hidden, 1, 0), 7: (hidden, 1, 1),
                     9: (outer, 0, 0), 11: (outer, 0, 1), 13: (outer, 1, 0), 16: (outer, 1, 1)}

            with pe.If(in_windows(pe)):
                def group(i, q):
                    pe.wait_ge(s_oneh[q], i + 1)
                    pe.wait_ge(s_low[q], i + 1)
                    if q >= PARTS:
                        pe.wait_ge(s_added[q - PARTS], i + 1)
                    elif later(i):
                        pe.wait_ge(s_added[q - PARTS], i)
                    else:
                        pe.wait_ge(s_idx_act, CH)
                    edge_sums(bank[q % PARTS], q).then_inc(s_esum[q], 1)

                def groups(i):
                    for q in range(SLOTS):
                        group(i, q)

                def span(k, i=None, pairs=SPAN, size=SPAN * SLOTS):
                    for j in range(SPAN * SLOTS):
                        if j < size:
                            group(*group_at(k, j))
                        if i is not None and j in parts:
                            part, a, b = parts[j]
                            part(i, a, b)
                        if j % SLOTS == SLOTS - 1 and j // SLOTS < pairs:
                            h0tr(SPAN * k + j // SLOTS)

                groups(0)
                loop(pe, groups, 1, H0[0])
                pe.wait_ge(s_w, 8 * 16)
                span(0)
                span(1, 0)
                loop(pe, lambda k: span(k, k - 1), 2, BODIES)
                span(BODIES, BODIES - 1, pairs=1, size=REMAIN)
            with pe.Else():
                pe.wait_ge(s_idx_act, CH)
                for c in range(CH):
                    if c >= 2:
                        pe.wait_ge(a_trc, c - 1)
                    transpose_table(pe, bank[c % 2], raw, c).then_inc(a_tr, 1)
                pe.wait_ge(a_trc, CH)
                h0tr(0)
                loop(pe, h0tr, 1, U)

                def any_group(g):
                    with pe.Fori(0, NW) as w:
                        pe.wait_ge(a_low, g + 1)
                        pe.wait_ge(a_oneh, g * NW + w + 1)
                        edge_sums(bank[0], 0).then_inc(a_sum, 1)

                loop(pe, any_group, 0, G)
                pe.wait_ge(s_w, 8 * 16)

                def any_layer0(i):
                    for part, a, b in parts.values():
                        part(i, a, b)

                any_layer0(0)
                loop(pe, any_layer0, 1, BESIDE)

            pe.wait_ge(s_acc, 1)
            for t in range(T):
                ins = pe.transpose(bank[0][:, t:t + 1], acc[FE:FE + 1, t * P:(t + 1) * P], ident[FE:FE + 1, FE:FE + 1])
            ins.then_inc(s_cntp, 1)
            pe.wait_ge(s_cnt, 1)
            pe.transpose(bank[1][0:T, 0:P], cntN[:, :], ident[:, :]).then_inc(s_cntT, 1)
            for k in range(2):
                pe.matmul(bank[0][:, 0:CB], below[:, k, :], cntN[:, :].rearrange("p (b k) -> p k b", k=2)[:, k, :],
                          start=(k == 0), stop=False)
            pe.wait_ge(s_totb, 1)
            pe.matmul(bank[0][:, 0:CB], ones[0:T, :], totb[:, :], start=False, stop=True).then_inc(s_startp, 1)

            def key_transposes(n, v, done):
                pe.wait_ge(s_keys, n + 1)
                if done is s_lotr:
                    pe.wait_ge(s_keyT, n + 1)
                elif later(n):
                    pe.wait_ge(s_loT, n)
                for j in range(KB):
                    ins = pe.transpose(bank16[:, j * P:(j + 1) * P], v[:, j * SL:(j + 1) * SL], ident16[:, :])
                ins.then_inc(done, 1)

            def layer0(i, n=None):
                for q in range(2):
                    for k in range(2):
                        hidden(i, q, k, own=1)
                if n is not None:
                    key_transposes(n, key16[n % 2], s_keytr)
                for q in range(2):
                    outer(i, q, 0)
                    outer(i, q, 1)
                if n is not None:
                    key_transposes(n, lo16[n % 2], s_lotr)

            pe.wait_ge(s_hids[1], 2 * BESIDE)
            pe.wait_ge(s_h0T, U)
            loop(pe, layer0, BESIDE, KEY0)
            for n in range(3):
                layer0(KEY0 + n, n)
            hidden(U // 2, 0, 0, own=1)
            hidden(U // 2, 0, 1, own=1)
            outer(U // 2, 0, 0)
            outer(U // 2, 0, 1)
            for n in (3, 4):
                key_transposes(n, key16[n % 2], s_keytr)
                key_transposes(n, lo16[n % 2], s_lotr)
            pe.wait_ge(s_x1[0], U // 2 + 1)
            pe.wait_ge(s_x1[1], U // 2)
            pe.wait_ge(s_hids[0], 2 * (U // 2) + 2)

            pe.wait_ge(s_nopl, 1)
            pe.matmul(bank[7][0:1, 0:CB // KB], ones[:, 0:1], noplace[:, :], start=True, stop=True).then_inc(s_noplp, 1)

            def couples(t, s):
                n = t * ST + s
                pe.wait_ge(s_one, n + 1)
                if isinstance(n, int) and n < 2:
                    pe.wait_ge(s_loT, CB // KB)
                else:
                    pe.wait_ge(s_adj, n - 1)
                q = s % 2
                for c in range(SC):
                    ins = pe.matmul(cpl[q][:, c // BC, (c % BC) * KEYS:(c % BC + 1) * KEYS], onesrc[:, q, c, :],
                                    onekey[:, q, c, :], start=True, stop=True)
                ins.then_inc(s_cplp, 1)

            def dense(t, par, h0_, h1_):
                for h in range(h0_, h1_):
                    ins = pe.matmul(bank[4 + par], adj[:, par, :, h], htab[:, h, :], start=(h == 0), stop=(h == TN - 1))
                return ins

            def transposes(t):
                pe.wait_ge(s_sumN, t + 1)
                pe.wait_ge(s_h1, t + 1)
                if later(t):
                    pe.wait_ge(s_trs, t)
                for k, v in enumerate((sumN, h1buf)):
                    for h in range(DH):
                        ins = pe.transpose(bank[6][:, (2 * k + h) * P:(2 * k + h + 1) * P], v[:, h * P:(h + 1) * P], ident[:, :])
                ins.then_inc(s_trp, 1)

            def products(t):
                pe.wait_ge(s_trs, t + 1)
                if later(t):
                    pe.wait_ge(s_res, t)
                for k, w in enumerate((wns, wss)):
                    for h in range(DH):
                        ins = pe.matmul(bank[7][:, k * D:(k + 1) * D], bothT[:, (2 * k + h) * P:(2 * k + h + 1) * P],
                                        w[:, h, :], start=(h == 0), stop=(h == DH - 1))
                ins.then_inc(s_outq, 1)

            for s in range(ST):
                couples(0, s)
            with pe.If(in_places(pe)):
                cut = [TN * s // ST for s in range(ST + 1)]

                def tile(t, par, first=False, last=False):
                    pe.wait_ge(s_adj, t * ST + ST)
                    if not first and not (isinstance(t, int) and t == 1):
                        pe.wait_ge(s_sumN, t - 1)
                    for s in range(ST):
                        if not last:
                            couples(t + 1, s)
                        ins = dense(t, par, cut[s], cut[s + 1])
                        if s == 2 and not first:
                            transposes(t - 1)
                        if s == 4 and not first:
                            products(t - 1)
                    ins.then_inc(s_dense, 1)

                tile(0, 0, first=True)
                tile(1, 1)
                tile(2, 0)
                with pe.Fori(0, TN // 4 - 1) as i:
                    for t in range(3, 7):
                        tile(4 * i + t, t % 2)
                tile(TN - 2, 1)
                tile(TN - 1, 0, last=True)
                transposes(TN - 1)
                products(TN - 1)
            with pe.Else():
                pe.wait_ge(s_adj, ST)
                for c in range(CH):
                    for k in range(2):
                        if c == 0:
                            pe.wait_ge(n_rawf, 1)
                        if c >= 2:
                            pe.wait_ge(n_trc, 2 * (c - 2) + k + 1)
                        transpose_table(pe, bank[2 * k + c % 2], raw1[:, k], c).then_inc(n_tr, 1)

                def self_part(t):
                    pe.wait_ge(n_h, t + 1)
                    if later(t):
                        pe.wait_ge(n_hTs, t)
                    for h in range(DH):
                        ins = pe.transpose(bank[4][:, h * P:(h + 1) * P], hbuf[:, 0, 0, h * P:(h + 1) * P], ident[:, :])
                    ins.then_inc(n_hT, 1)
                    pe.wait_ge(n_hTs, t + 1)
                    if later(t):
                        pe.wait_ge(n_self, t)
                    for h in range(DH):
                        ins = pe.matmul(bank[5][:, 0:D], hbuf[:, 0, 1, h * P:(h + 1) * P], wss[:, h, :],
                                        start=(h == 0), stop=(h == DH - 1))
                    ins.then_inc(n_selfp, 1)

                self_part(0)
                loop(pe, self_part, 1, TN)
                pe.wait_ge(n_trc, 2 * CH)

                def any_sums(g):
                    with pe.Fori(0, NW) as w:
                        pe.wait_ge(n_rows, 16 * CH * (g + 1))
                        pe.wait_ge(n_oneb, g * NW + w + 1)
                        for h in range(DH):
                            for c in range(CH):
                                for k in range(2):
                                    ins = pe.matmul(bank[0][:, h * WIN:(h + 1) * WIN],
                                                    rows[:, c, k * D + h * P:k * D + (h + 1) * P], oneb[:, c, :],
                                                    start=(c == 0 and k == 0), stop=(c == CH - 1 and k == 1))
                        ins.then_inc(n_sum, 1)

                loop(pe, any_sums, 0, G)

                def neigh(t):
                    pe.wait_ge(n_sumc, t + 1)
                    if later(t):
                        pe.wait_ge(n_res, t)
                    for h in range(DH):
                        ins = pe.matmul(bank[6][:, 0:D], hids[:, 0, 0, h * P:(h + 1) * P], wns[:, h, :],
                                        start=(h == 0), stop=(h == DH - 1))
                    ins.then_inc(n_neighp, 1)

                neigh(0)
                loop(pe, neigh, 1, TN)

        @block.vector
        def _(dve):
            dve.wait_ge(s_raw, 5 * 16)
            for b, m in ((0, G0), (1, G1)):
                dve.tensor_copy(raw[0:m, b, :], rawi[0:m, b, :])
            dve.drain()
            for b, m in ((0, G0), (1, G1)):
                ins = dve.tensor_scalar(relr[0:m, b, :], raw[0:m, b, :], raw[0:m, b, 0:1], None, ALU.subtract)
            ins.then_inc(s_rel, 1)
            dve.wait_ge(s_const, 1)
            dve.drain()
            for b, m in ((0, G0), (1, G1)):
                dve.tensor_reduce(viol[0:m, 2 * b + 1:2 * b + 2], relr[0:m, b, :], AX.X, ALU.max)
                dve.tensor_reduce(viol[0:m, 2 * b + 2:2 * b + 3], relr[0:m, b, :], AX.X, ALU.min)
                dve.tensor_tensor(viol[0:m, 8 + b:9 + b], limit[0:m, b:b + 1], raw[0:m, b, 0:1], ALU.subtract)
            dve.drain()
            dve.tensor_scalar(viol[:, 5:6], viol[:, 1:2], viol[:, 3:4], float(WIN - 1), ALU.max, ALU.subtract)
            dve.tensor_scalar(viol[:, 6:7], viol[:, 2:3], viol[:, 4:5], -1.0, ALU.min, ALU.mult)
            dve.drain()
            dve.tensor_tensor(viol[:, 7:8], viol[:, 5:6], viol[:, 6:7], ALU.max)
            dve.tensor_tensor(viol[:, 10:11], viol[:, 8:9], viol[:, 9:10], ALU.max)
            dve.drain()
            dve.tensor_tensor(viol[:, 0:1], viol[:, 7:8], viol[:, 10:11], ALU.max).then_inc(s_viol, 1)
            dve.wait_ge(s_violT, 1)
            dve.tensor_reduce(viol[0:1, 7:8], bank[7][0:1, 0:P], AX.X, ALU.max)
            dve.drain()
            dve.tensor_scalar(flag[0:1, 0:1], viol[0:1, 7:8], 0.0, 1.0, ALU.max, ALU.min).then_inc(s_flag, 1)

            def layernorm0():
                dve.wait_ge(s_sd0, 1)
                dve.reciprocal(ln0[:, 4, :], ln0[:, 3, :])
                dve.drain()
                dve.tensor_tensor(ln0[:, 5, :], ln0[:, 4, :], ln0[:, 1, :], ALU.mult).then_inc(s_ln0, 1)

            def add_window(into, start, part):
                v = into[..., bass.ds(start, WIN)]
                return dve.tensor_tensor(v, v, part, ALU.add)

            def in_window(o, rel):
                return dve.tensor_tensor(o, iota[:, :].unsqueeze(1).broadcast_to([P, CH, WIN]),
                                         rel.unsqueeze(2).broadcast_to([P, CH, WIN]), ALU.is_equal)

            def inverse(i, q, half):
                v = deg[:, half * P:(half + 1) * P]
                dve.tensor_scalar(v, acc[FE:P, bass.ds((2 * i + q) * NM + half * P, P)], 1.0, None, ALU.max)
                dve.drain()
                dve.reciprocal(v, v)

            def mean_edges(i, q):
                dve.drain()
                if later(i):
                    dve.wait_ge(s_hidp[q], 2 * i)
                dve.tensor_tensor(aggn[:, q, :], acc[0:FE, bass.ds((2 * i + q) * NM, NM)], deg[:, :],
                                  ALU.mult).then_inc(s_agg[q], 1)

            def add_x(i, q):
                v = xr[:, bass.ds(2 * (2 * i + q), 2), :]
                dve.wait_ge(s_b2, 2 * i + q + 1)
                dve.wait_ge(s_outp[q], i + 1)
                dve.tensor_tensor(v, v, bank[6 + q][:, :].rearrange("p (t d) -> p t d", t=2), ALU.add).then_inc(s_x1[q], 1)

            def stats(i, q):
                dve.drain()
                for t in range(2):
                    dve.bn_stats(st6[:, q, t, :], tile_of(xr, 2 * (2 * i + q) + t))
                dve.drain()

            def variance(i, q):
                dve.drain()
                for t in range(2):
                    dve.bn_aggr(mv[:, q, t, :], st6[:, q, t, :])
                dve.drain()
                dve.tensor_scalar(ve[:, q, :], mv[:, q, :, 1], EPS, None, ALU.add).then_inc(s_var1[q], 1)

            def x1_stats(i, q):
                add_x(i, q)
                stats(i, q)
                variance(i, q)

            def ln1(i, q):
                dve.wait_ge(s_sd1[q], i + 1)
                dve.reciprocal(sd[:, q, :], sd[:, q, :])
                dve.drain()
                dve.tensor_scalar(rsq[:, q, :], sd[:, q, :], SCALE, None, ALU.mult)
                dve.scalar_tensor_tensor(nmq[:, q, :], mv[:, q, :, 0], -SCALE, sd[:, q, :], ALU.mult,
                                         ALU.mult).then_inc(s_ln1[q], 1)

            def low_part(i, q):
                u = 2 * i + q
                dve.wait_ge(s_hi[q], i + 1)
                dve.tensor_tensor(htab[:, bass.ds(2 * u, 2), D:2 * D], hbuf[:, q, :, :], htab[:, bass.ds(2 * u, 2), 0:D],
                                  ALU.subtract).then_inc(s_tab[q], 1)

            def all_means(i, q):
                dve.drain()
                inverse(i, q, 0)
                inverse(i, q, 1)
                mean_edges(i, q)

            def keys(n):
                frm = kreg[:, 1, bass.ds(n * KB, KB), :].rearrange("p b s -> p (b s)")
                dve.wait_ge(s_places, 16 * 2 * KB * (n + 1))
                dve.drain()
                if n >= 2:
                    dve.wait_ge(s_lotr, n - 1)
                dve.tensor_tensor(key.rearrange("p (b s) -> p b s", b=KB), kreg[:, 0, bass.ds(n * KB, KB), :],
                                  node0[:, bass.ds(n * KB, KB)].unsqueeze(2).broadcast_to([P, KB, SL]), ALU.subtract)
                dve.tensor_scalar(khi, frm, 7, None, ALU.arith_shift_right)
                dve.drain()
                dve.scalar_tensor_tensor(away, key, -1.0, key, ALU.add, ALU.mult)
                dve.scalar_tensor_tensor(lo16[n % 2], khi, -float(P), frm, ALU.mult, ALU.add)
                dve.scalar_tensor_tensor(key, key, float(TN), khi, ALU.mult, ALU.add)
                dve.drain()
                dve.tensor_scalar(away, away, 0.5, NOKEY, ALU.is_gt, ALU.mult)
                dve.drain()
                dve.tensor_reduce(noplace[:, bass.ds(n, 1)], away, AX.X, ALU.add)
                dve.scalar_tensor_tensor(key16[n % 2], key, NOKEY, away, ALU.min, ALU.max).then_inc(s_keys, 1)

            def layer0(i, n=None, last=False):
                all_means(i + 1, 0)
                if not last:
                    all_means(i + 1, 1)
                x1_stats(i, 0)
                x1_stats(i, 1)
                ln1(i, 0)
                ln1(i, 1)
                if n is not None:
                    keys(n)
                low_part(i, 0)
                low_part(i, 1)

            parts = [(0, 2, ln1, 0), (1, 0, inverse, 0, 0), (2, 2, add_x, 1), (3, 2, low_part, 0), (4, 2, stats, 1),
                     (5, 2, variance, 1), (6, 2, ln1, 1), (7, 0, inverse, 0, 1), (8, 0, mean_edges, 0),
                     (9, 2, low_part, 1), (10, 0, inverse, 1, 0), (12, 0, inverse, 1, 1), (13, 0, mean_edges, 1),
                     (15, 1, add_x, 0), (16, 1, stats, 0), (17, 1, variance, 0)]

            dve.wait_ge(s_const, 2)
            dve.wait_ge(s_masked, 1)
            def rest_of(q):
                return dve.tensor_tensor(rest[:, q % PARTS, :, :], edg[:, q, :, :], edg_top[:, q, :, :], ALU.subtract)

            with dve.If(in_windows(dve)):
                def prepare(i, q):
                    dve.wait_ge(s_edges[q], 16 * (i + 1))
                    rest_of(q).then_inc(s_rest[q], 1)
                    pairs = tile_pairs(relP, SLOTS * i + q)
                    dve.tensor_tensor(oneh[:, q % PARTS, :, :].rearrange("p c (v d) -> p c v d", d=2),
                                      iota16[:, 0:WIN].rearrange("p (v d) -> p v d", d=2).unsqueeze(1)
                                      .broadcast_to([P, CH, WIN // 2, 2]),
                                      pairs.unsqueeze(2).broadcast_to([P, CH, WIN // 2, 2]),
                                      ALU.is_equal).then_inc(s_oneh[q], 1)

                def start_of(i, q):
                    return dve.value_load(base[0:1, bass.ds(SLOTS * i + q, 1)], min_val=0, max_val=N - 1)

                def add(i, q, start=None):
                    if start is None:
                        start = start_of(i, q)
                    dve.wait_ge(s_esum[q], i + 1)
                    if q > 0:
                        dve.wait_ge(s_added[q - 1], i + 1)
                    elif later(i):
                        dve.wait_ge(s_added[SLOTS - 1], i)
                    add_window(acc[:, :], start, bank[q % PARTS][:, 0:WIN]).then_inc(s_added[q], 1)

                def step(i, q, between=()):
                    prepare(i, q)
                    due = (i, q - LAG) if q >= LAG else (i - 1, q + SLOTS - LAG) if later(i) else None
                    start = due and start_of(*due)
                    for part, *which in between:
                        part(*which)
                    if due:
                        add(*due, start)

                def slots(i):
                    for q in range(SLOTS):
                        step(i, q)

                slots(0)
                loop(dve, slots, 1, H0[0])
                layernorm0()

                def span(k, size=SPAN * SLOTS):
                    for j in range(SPAN * SLOTS):
                        between = [(part, k - back, *which) for at, back, part, *which in parts
                                   if at == j and (not isinstance(k, int) or k >= back)]
                        if j < size:
                            step(*group_at(k, j), between)
                        else:
                            for part, *which in between:
                                part(*which)

                for k in range(3):
                    span(k)
                loop(dve, span, 3, BODIES)
                span(BODIES, size=REMAIN)
                for q in range(TAIL - LAG, TAIL):
                    add(FULL, q)
                dve.drain()
                dve.nop().then_inc(s_acc, 1)
                ln1(BODIES - 1, 0)
                low_part(BODIES - 1, 0)
                x1_stats(BODIES - 1, 1)
                ln1(BODIES - 1, 1)
                low_part(BODIES - 1, 1)
            with dve.Else():
                layernorm0()
                dve.wait_ge(s_masked, 2)

                def any_group(g):
                    if later(g):
                        dve.wait_ge(a_edges, 16 * g)
                    else:
                        dve.wait_ge(s_edges[0], 16)
                    rest_of(0).then_inc(a_rest, 1)
                    dve.memset(wstart[:, :], 0.0)
                    dve.drain()
                    with dve.Fori(0, NW) as w:
                        dve.tensor_scalar(relw[:, :], tile_of(dstT0, g), wstart[:, 0:1], None, ALU.subtract)
                        dve.drain()
                        dve.tensor_scalar(wstart[:, :], wstart[:, :], float(WIN), None, ALU.add)
                        in_window(oneh[:, 0, :, :], relw[:, :]).then_inc(a_oneh, 1)
                        dve.wait_ge(a_sum, g * NW + w + 1)
                        add_window(acc[:, :], w * WIN, bank[0][:, 0:WIN])
                        dve.drain()
                    dve.nop().then_inc(a_group, 1)

                any_group(0)
                loop(dve, any_group, 1, G)
                all_means(0, 0)
                all_means(0, 1)
                layer0(0)
                loop(dve, layer0, 1, BESIDE)
                dve.drain()
                dve.nop().then_inc(s_acc, 1)

            dve.wait_ge(s_cntp, 1)
            dve.tensor_copy(cntN[:, :], bank[0][:, 0:T]).then_inc(s_cnt, 1)
            dve.wait_ge(s_cntT, 1)
            dve.tensor_reduce(tot[:, :], bank[1][0:T, 0:P], AX.X, ALU.add)
            dve.tensor_scalar(invT[:, :], cntN[:, :], 1.0, None, ALU.max)
            dve.drain()
            dve.tensor_scalar(totb[:, :], tiles_before[:, :], tot[:, 0:1], None, ALU.mult).then_inc(s_totb, 1)
            dve.reciprocal(invT[:, :], invT[:, :])
            dve.wait_ge(s_startp, 1)
            dve.tensor_scalar(startu[:, :], bank[0][:, 0:CB], float(E - SL), None, ALU.min).then_inc(s_start, 1)
            dve.drain()
            dve.tensor_scalar(invT[:, :], invT[:, :], 1.0 / SCALE, None, ALU.mult)

            for n in range(4):
                layer0(BESIDE + n, n, last=(n == 3))
            keys(4)
            x1_stats(U // 2, 0)
            ln1(U // 2, 0)
            low_part(U // 2, 0)
            dve.drain()
            dve.nop().then_inc(s_nopl, 1)
            def twice(n, k):
                return pairs16[:, k, bass.ds(n * SC, SC), :]

            def one_hots(t, s):
                n = t * ST + s
                q = s % 2
                if not isinstance(n, int) or n >= 2:
                    dve.wait_ge(s_cplp, n - 1)
                for o, k, size in ((onesrc, 1, P), (onekey, 0, KEYS)):
                    ins = dve.tensor_tensor(o[:, q, :, :].rearrange("p c (v d) -> p c v d", d=2),
                                            iota16[:, 0:size].rearrange("p (v d) -> p v d", d=2).unsqueeze(1)
                                            .broadcast_to([P, SC, size // 2, 2]),
                                            twice(n, k).unsqueeze(2).broadcast_to([P, SC, size // 2, 2]), ALU.is_equal)
                ins.then_inc(s_one, 1)

            dve.wait_ge(s_loT, 1)
            for s in range(ST):
                one_hots(0, s)
            dve.wait_ge(s_loT, CB // KB)

            dve.wait_ge(s_noplp, 1)
            dve.tensor_reduce(viol[0:1, 1:2], bank[7][0:1, 0:CB // KB], AX.X, ALU.add)
            dve.drain()
            dve.tensor_scalar(flag[0:1, 1:2], viol[0:1, 1:2], NOKEY * (CB * P * SL - E), 1.0, ALU.not_equal,
                              ALU.mult).then_inc(s_flag1, 1)

            with dve.If(in_places(dve)):
                def sum_parts(t, par):
                    dve.wait_ge(s_dense, t + 1)
                    if later(t):
                        dve.wait_ge(s_trp, t)
                    dve.tensor_copy(sumN[:, :], bank[4 + par][:, 0:D])
                    dve.drain()
                    dve.tensor_tensor(sumN[:, :], sumN[:, :], bank[4 + par][:, D:2 * D], ALU.add).then_inc(s_sumN, 1)

                def result(t, i, q):
                    dve.wait_ge(s_outq, t + 1)
                    dve.wait_ge(s_bs, t + 1)
                    if later(i):
                        dve.wait_ge(s_out[q], 16 * i)
                    dve.scalar_tensor_tensor(finished[q], bank[7][:, D:2 * D], 1.0 / SCALE, tile_of(xr, t), ALU.mult, ALU.add)
                    dve.drain()
                    dve.scalar_tensor_tensor(finished[q], bank[7][:, 0:D], invT[:, bass.ds(t, 1)], finished[q],
                                             ALU.mult, ALU.add).then_inc(s_res, 1)

                def tile(t, i, par, first=False, last=False):
                    for s in range(ST):
                        if not last:
                            one_hots(t + 1, s)
                        if s == 1 and not first:
                            sum_parts(t - 1, 1 - par)
                        if s == 6 and not first:
                            result(t - 1, i, 1 - par)

                tile(0, 0, 0, first=True)
                tile(1, 0, 1)
                tile(2, 0, 0)
                with dve.Fori(0, TN // 4 - 1) as i:
                    for t in range(3, 7):
                        tile(4 * i + t, 2 * i + (t - 1) // 2, t % 2)
                tile(TN - 2, TN // 2 - 1, 1)
                tile(TN - 1, TN // 2 - 1, 0, last=True)
                sum_parts(TN - 1, 0)
                result(TN - 1, TN // 2, 0)
            with dve.Else():
                dve.wait_ge(n_table, 16)
                dve.memset(sumT, 0.0)
                dve.wait_ge(n_raw, 6 * 16)
                for k in range(2):
                    for b, m in ((0, G0), (1, G1)):
                        dve.tensor_copy(raw1[0:m, k, b, :], raw1i[0:m, k, b, :])
                dve.drain()
                dve.nop().then_inc(n_rawf, 1)

                def self_add(t):
                    dve.wait_ge(n_selfp, t + 1)
                    v = tile_of(xr, t)
                    dve.scalar_tensor_tensor(v, bank[5][:, 0:D], 1.0 / SCALE, v, ALU.mult, ALU.add).then_inc(n_self, 1)
                    dve.drain()
                    dve.tensor_tensor(v, v, bsbc[:, :], ALU.add)

                loop(dve, self_add, 0, TN)
                dve.wait_ge(s_masked, 3)
                with dve.Fori(0, G) as g:
                    dve.memset(wstart[:, :], 0.0)
                    dve.drain()
                    with dve.Fori(0, NW) as w:
                        dve.tensor_scalar(relw[:, :], tile_of(dstT1, g), wstart[:, 0:1], None, ALU.subtract)
                        dve.drain()
                        dve.tensor_scalar(wstart[:, :], wstart[:, :], float(WIN), None, ALU.add)
                        in_window(oneb, relw[:, :]).then_inc(n_oneb, 1)
                        dve.wait_ge(n_sum, g * NW + w + 1)
                        add_window(sumT, w * WIN, bank[0][:, 0:DH * WIN].rearrange("p (h w) -> p h w", h=DH))
                        dve.drain()
                    dve.nop().then_inc(n_group, 1)
                dve.drain()
                dve.nop().then_inc(n_done, 1)

                def any_result(t):
                    dve.wait_ge(n_neighp, t + 1)
                    if later(t):
                        dve.wait_ge(n_out, 16 * t)
                    dve.scalar_tensor_tensor(hbuf[:, 0, 0, :], bank[6][:, 0:D], invT[:, bass.ds(t, 1)], tile_of(xr, t),
                                             ALU.mult, ALU.add).then_inc(n_res, 1)

                any_result(0)
                loop(dve, any_result, 1, TN)


_INS = ["x", "src", "dst", "edge_attr_64", "L0_gnn_W1", "L0_gnn_b1", "L0_gnn_W2", "L0_gnn_b2",
        "L1_gnn_w_neigh", "L1_gnn_w_self", "L1_gnn_b_self"]
_TRANSPOSED = ("L1_gnn_w_neigh", "L1_gnn_w_self")


def kernel(**inputs):
    import numpy as _np
    import concourse.bacc as _bacc
    from concourse import mybir as _mybir
    from concourse.bass_utils import run_bass_kernel_spmd as _run

    nc = _bacc.Bacc("TRN2", target_bir_lowering=False, num_devices=1)
    arrays, args = {}, []
    for name in _INS:
        a = _np.asarray(inputs[name])
        a = _np.ascontiguousarray(a.T if name in _TRANSPOSED else a)
        arrays[f"in_{name}_dram"] = a
        args.append(nc.dram_tensor(f"in_{name}_dram", a.shape, _mybir.dt.from_np(a.dtype), kind="ExternalInput").ap())
    n, d = inputs["x"].shape
    out = nc.dram_tensor("out_dram", (n, d), _mybir.dt.float32, kind="ExternalOutput").ap()
    gnn_kernel(nc, *args, out)
    r = _run(nc, [arrays], core_ids=[0])
    return r.results[0]["out_dram"]
```
